# Optimizing a Trainium2 kernel written in Bass

```python
import numpy as np
import jax
import jax.numpy as jnp

def _softmax(x, axis=-1):
    return jax.nn.softmax(x, axis=axis)

def _gelu(x):
    return jax.nn.gelu(x, approximate=True)

def _silu(x):
    return jax.nn.silu(x)

def _sigmoid(x):
    return jax.nn.sigmoid(x)

def _layernorm(x, axis=-1, eps=1e-05):
    m = jnp.mean(x, axis=axis, keepdims=True)
    v = jnp.var(x, axis=axis, keepdims=True)
    return (x - m) / jnp.sqrt(v + eps)

def _scatter_add(tgt, idx, src, axis=0):
    return tgt.at[idx].add(src)

def _segment_sum(src, seg, n):
    return jax.ops.segment_sum(src, seg, n)
kernel_name = 'mk_xattn_seq_d1_seqx_r4_994c63'

def setup_inputs(seed: int=0):
    np.random.seed(seed)
    _w = jnp.asarray

    def _rec_inputs():
        import jax
        import jax.numpy as jnp
        _rk = jax.random.key(seed)
        x = -0.0002928 + 1 * jax.random.normal(jax.random.fold_in(_rk, 1), (4, 1024, 256), jnp.float32)
        _lenS = 1024 - jax.random.randint(jax.random.fold_in(_rk, 7), (4,), 0, max(1, 1024 // 4) + 1, jnp.int32)
        _lenS2 = 154 - jax.random.randint(jax.random.fold_in(_rk, 8), (4,), 0, max(1, 154 // 4) + 1, jnp.int32)
        _ctx_1024P = jax.random.normal(jax.random.fold_in(_rk, 11), (4, 16, 256), jnp.float32)
        _ctx_1024c = jax.random.dirichlet(jax.random.fold_in(_rk, 511), 0.3 * jnp.ones((16,), jnp.float32), (4, 154))
        _ctx_1024t = jnp.einsum('bsk,bkd->bsd', _ctx_1024c, _ctx_1024P)
        _ctx_1024t = _ctx_1024t * jax.lax.rsqrt(jnp.mean(jnp.square(_ctx_1024t)) + 1e-12) * 0.953939
        ctx_1024 = -1.39393e-06 + 0.999914 * (_ctx_1024t + 0.3 * jax.random.normal(jax.random.fold_in(_rk, 611), (4, 154, 256), jnp.float32))
        return (x, ctx_1024)
    x, ctx_1024 = _rec_inputs()

    def _L0_xattn_setup():
        import jax, jax.numpy as jnp
        import numpy as np
        D_MODEL = 256
        N_HEADS = 16
        D_K = D_MODEL // N_HEADS
        D_FFN = 1024
        EPS = 1e-06
        NEG_INF = -1000000000.0

        def _ln(x, scale, bias):
            mu = jnp.mean(x, axis=-1, keepdims=True)
            var = jnp.mean(jnp.square(x - mu), axis=-1, keepdims=True)
            return (x - mu) * jax.lax.rsqrt(var + EPS) * scale + bias

        def _attend(q, k, v, mask):
            scale = jax.lax.rsqrt(jnp.asarray(D_K, q.dtype))
            logits = jnp.einsum('bhqd,bhkd->bhqk', q, k) * scale
            if mask is not None:
                logits = jnp.where(mask, logits, jnp.asarray(NEG_INF, logits.dtype))
            w = jax.nn.softmax(logits.astype(jnp.float32), axis=-1).astype(q.dtype)
            return jnp.einsum('bhqk,bhkd->bhqd', w, v)

        def _heads(t, B, L):
            return jnp.transpose(t.reshape(B, L, N_HEADS, D_K), (0, 2, 1, 3))
        key = jax.random.key(seed)
        ks = jax.random.split(key, 16)
        B, L = (2, 512)
        s = lambda fan_in: 1.0 / np.sqrt(fan_in)
        return {'x': jax.random.normal(ks[0], (B, L, D_MODEL), jnp.float32), 'encoder_output': jax.random.normal(ks[1], (B, L, D_MODEL), jnp.float32), 'W_qkv': jax.random.normal(ks[2], (D_MODEL, 3 * D_MODEL), jnp.float32) * s(D_MODEL), 'W_self_out': jax.random.normal(ks[3], (D_MODEL, D_MODEL), jnp.float32) * s(D_MODEL), 'W_q': jax.random.normal(ks[4], (D_MODEL, D_MODEL), jnp.float32) * s(D_MODEL), 'W_kv': jax.random.normal(ks[5], (D_MODEL, 2 * D_MODEL), jnp.float32) * s(D_MODEL), 'W_cross_out': jax.random.normal(ks[6], (D_MODEL, D_MODEL), jnp.float32) * s(D_MODEL), 'W1': jax.random.normal(ks[7], (D_MODEL, D_FFN), jnp.float32) * s(D_MODEL), 'b1': jnp.zeros((D_FFN,), jnp.float32), 'W2': jax.random.normal(ks[8], (D_FFN, D_MODEL), jnp.float32) * s(D_FFN), 'b2': jnp.zeros((D_MODEL,), jnp.float32), 'ln1_scale': jnp.ones((D_MODEL,), jnp.float32), 'ln1_bias': jnp.zeros((D_MODEL,), jnp.float32), 'ln2_scale': jnp.ones((D_MODEL,), jnp.float32), 'ln2_bias': jnp.zeros((D_MODEL,), jnp.float32), 'ln3_scale': jnp.ones((D_MODEL,), jnp.float32), 'ln3_bias': jnp.zeros((D_MODEL,), jnp.float32)}
    _L0_xattn_all = _L0_xattn_setup()
    _L0_xattn_in = {k: v for k, v in _L0_xattn_all.items() if k in ('W_qkv', 'W_self_out', 'W_q', 'W_kv', 'W_cross_out', 'W1', 'b1', 'W2', 'b2', 'ln1_scale', 'ln1_bias', 'ln2_scale', 'ln2_bias', 'ln3_scale', 'ln3_bias')}
    del _L0_xattn_all
    return {'x': x, 'ctx_1024': ctx_1024, 'L0_xattn_W_qkv': _L0_xattn_in['W_qkv'], 'L0_xattn_W_self_out': _L0_xattn_in['W_self_out'], 'L0_xattn_W_q': _L0_xattn_in['W_q'], 'L0_xattn_W_kv': _L0_xattn_in['W_kv'], 'L0_xattn_W_cross_out': _L0_xattn_in['W_cross_out'], 'L0_xattn_W1': _L0_xattn_in['W1'], 'L0_xattn_b1': _L0_xattn_in['b1'], 'L0_xattn_W2': _L0_xattn_in['W2'], 'L0_xattn_b2': _L0_xattn_in['b2'], 'L0_xattn_ln1_scale': _L0_xattn_in['ln1_scale'], 'L0_xattn_ln1_bias': _L0_xattn_in['ln1_bias'], 'L0_xattn_ln2_scale': _L0_xattn_in['ln2_scale'], 'L0_xattn_ln2_bias': _L0_xattn_in['ln2_bias'], 'L0_xattn_ln3_scale': _L0_xattn_in['ln3_scale'], 'L0_xattn_ln3_bias': _L0_xattn_in['ln3_bias']}

def reference(x, ctx_1024, L0_xattn_W_qkv, L0_xattn_W_self_out, L0_xattn_W_q, L0_xattn_W_kv, L0_xattn_W_cross_out, L0_xattn_W1, L0_xattn_b1, L0_xattn_W2, L0_xattn_b2, L0_xattn_ln1_scale, L0_xattn_ln1_bias, L0_xattn_ln2_scale, L0_xattn_ln2_bias, L0_xattn_ln3_scale, L0_xattn_ln3_bias):
    import jax
    import jax.numpy as jnp

    def _L0_xattn_ref(x, encoder_output, W_qkv, W_self_out, W_q, W_kv, W_cross_out, W1, b1, W2, b2, ln1_scale, ln1_bias, ln2_scale, ln2_bias, ln3_scale, ln3_bias):
        import jax, jax.numpy as jnp
        import numpy as np
        D_MODEL = 256
        N_HEADS = 16
        D_K = D_MODEL // N_HEADS
        D_FFN = 1024
        EPS = 1e-06
        NEG_INF = -1000000000.0

        def _ln(x, scale, bias):
            mu = jnp.mean(x, axis=-1, keepdims=True)
            var = jnp.mean(jnp.square(x - mu), axis=-1, keepdims=True)
            return (x - mu) * jax.lax.rsqrt(var + EPS) * scale + bias

        def _attend(q, k, v, mask):
            scale = jax.lax.rsqrt(jnp.asarray(D_K, q.dtype))
            logits = jnp.einsum('bhqd,bhkd->bhqk', q, k) * scale
            if mask is not None:
                logits = jnp.where(mask, logits, jnp.asarray(NEG_INF, logits.dtype))
            w = jax.nn.softmax(logits.astype(jnp.float32), axis=-1).astype(q.dtype)
            return jnp.einsum('bhqk,bhkd->bhqd', w, v)

        def _heads(t, B, L):
            return jnp.transpose(t.reshape(B, L, N_HEADS, D_K), (0, 2, 1, 3))
        B, L, _ = x.shape
        Ls = encoder_output.shape[1]
        nx = _ln(x, ln1_scale, ln1_bias)
        qkv = nx @ W_qkv
        q, k, v = (_heads(qkv[..., i * D_MODEL:(i + 1) * D_MODEL], B, L) for i in range(3))
        causal = jnp.tril(jnp.ones((L, L), jnp.bool_))[None, None]
        ctx = _attend(q, k, v, causal)
        attn = jnp.transpose(ctx, (0, 2, 1, 3)).reshape(B, L, D_MODEL) @ W_self_out
        x = x + attn
        nx = _ln(x, ln2_scale, ln2_bias)
        q = _heads(nx @ W_q, B, L)
        kv = encoder_output @ W_kv
        k = _heads(kv[..., :D_MODEL], B, Ls)
        v = _heads(kv[..., D_MODEL:], B, Ls)
        ctx = _attend(q, k, v, None)
        attn = jnp.transpose(ctx, (0, 2, 1, 3)).reshape(B, L, D_MODEL) @ W_cross_out
        x = x + attn
        nx = _ln(x, ln3_scale, ln3_bias)
        ffn = jax.nn.relu(nx @ W1 + b1) @ W2 + b2
        return x + ffn
    x = _L0_xattn_ref(x, ctx_1024, L0_xattn_W_qkv, L0_xattn_W_self_out, L0_xattn_W_q, L0_xattn_W_kv, L0_xattn_W_cross_out, L0_xattn_W1, L0_xattn_b1, L0_xattn_W2, L0_xattn_b2, L0_xattn_ln1_scale, L0_xattn_ln1_bias, L0_xattn_ln2_scale, L0_xattn_ln2_bias, L0_xattn_ln3_scale, L0_xattn_ln3_bias)
    return x

_drawn_inputs = setup_inputs


def setup_inputs(seed=0):
    import zlib

    import numpy as np

    out = dict(_drawn_inputs(seed))
    spreads = {'L0_xattn_b1': (0.0, 0.1),
     'L0_xattn_b2': (0.0, 0.1),
     'L0_xattn_ln1_scale': (1.0, 0.2),
     'L0_xattn_ln1_bias': (0.0, 0.1),
     'L0_xattn_ln2_scale': (1.0, 0.2),
     'L0_xattn_ln2_bias': (0.0, 0.424),
     'L0_xattn_ln3_scale': (1.0, 0.2),
     'L0_xattn_ln3_bias': (0.0, 0.1)}
    factors = {}
    for name, (base, spread) in spreads.items():
        noise = np.random.default_rng([zlib.crc32(name.encode()), seed]).standard_normal(out[name].shape)
        drawn = base * np.exp(spread * noise) if base else spread * noise
        out[name] = jnp.asarray(drawn.astype(out[name].dtype))
    for name, factor in factors.items():
        out[name] = (out[name] * factor).astype(out[name].dtype)
    return out
```

```python
from contextlib import ExitStack

import concourse.bass as bass
from concourse import mybir

ALU = mybir.AluOpType
ACT = mybir.ActivationFunctionType
AX = mybir.AxisListType
F32 = mybir.dt.float32
BF16 = mybir.dt.bfloat16

P = 128
EPS = 1e-6
MASKED = -1e30
LOWEST = -3e38


def decoder_block_kernel(
    nc, x, ctx_in, w_qkv, w_self_out, w_q, w_kv, w_cross_out, w1, b1, w2, b2,
    ln1_s, ln1_b, ln2_s, ln2_b, ln3_s, ln3_b, out,
):
    B, L, D = x.shape
    LX = ctx_in.shape[1]
    F = w1.shape[1]
    H, DK = 16, 16
    SCALE = float(DK) ** -0.5
    KC = D // P
    FC = F // P
    HF = 512
    TT = HF // P
    NV = DK + 1
    KPX = LX // 2
    NPART = 3
    Q_PARTS, K_PARTS = (0, 0, 0, 1, 1, 2), (0, 1, 2, 0, 1, 0)
    NPROD = len(Q_PARTS)
    KROWS = NPROD * DK
    SROWS = KROWS + NPART

    def dram(name, shape, dt):
        return nc.dram_tensor(name, shape, dt, kind="Internal").ap()

    q_parts = dram("q_parts", (2 * B, NPART, P, L), BF16)
    k_parts = dram("k_parts", (2 * B, NPART, P, L), BF16)
    v_aug = dram("v_aug", (B, L, H * NV), F32)
    qx_parts = dram("qx_parts", (2 * B, NPART, P, L), BF16)
    kx_parts = dram("kx_parts", (2 * B, NPART, P, LX), BF16)
    vx_aug = dram("vx_aug", (B, LX, H * NV), F32)
    self_ctx = dram("self_ctx", (2 * B, P, L), F32)
    cross_ctx = dram("cross_ctx", (2 * B, P, L), F32)
    x1_dram = dram("x1_dram", (B, L, D), F32)
    max_rows = dram("max_rows", (2, NPART, 32, P), BF16)

    def one(ap, i):
        return ap[bass.ds(i, 1)]

    def tokens(ap, b, hf):
        return one(ap, b).rearrange("b (h t p) d -> p (b h) t d", p=P, t=TT)[:, hf]

    with ExitStack() as ctx:
        def sb(name, shape, dt=F32):
            return ctx.enter_context(nc.sbuf_tensor(name, shape, dt))

        def sem(name):
            return ctx.enter_context(nc.semaphore(name))

        bank = ctx.enter_context(nc.psum_tensor("bank", [P, 8, HF], F32))

        wqkv_sb = sb("wqkv_sb", [P, KC, 3 * D])
        wso_sb = sb("wso_sb", [P, KC, D])
        wq_sb = sb("wq_sb", [P, KC, D])
        wkv_sb = sb("wkv_sb", [P, KC, 2 * D])
        wco_sb = sb("wco_sb", [P, KC, D])
        w1_sb = sb("w1_sb", [P, KC, F])
        w2_sb = sb("w2_sb", [P, FC, D])
        b1_sb = sb("b1_sb", [P, FC])
        b2_sb = sb("b2_sb", [P, D])
        lns_sb = sb("lns_sb", [P, 3, KC])
        lnb_sb = sb("lnb_sb", [P, 3, KC])
        ident = sb("ident", [P, P])
        ident_bf = sb("ident_bf", [P, P], BF16)
        causal_bf = sb("causal_bf", [P, P], BF16)
        minus_half = sb("minus_half", [P, TT])
        eps_sb = sb("eps_sb", [P, TT])

        xt = sb("xt", [P, 2, TT, D])
        out_mem = sb("out_mem", [P, 3 * 2 * HF])
        nx_mem = sb("nx_mem", [P, 2 * (L // P) * 8 * NV])
        vst_mem = sb("vst_mem", [P, 2 * TT * H * NV])
        xn = out_mem[:, 0:2 * TT * D].rearrange("p (h t d) -> p h t d", h=2, t=TT)
        nx = nx_mem[:, 0:2 * TT * D].rearrange("p (h t d) -> p h t d", h=2, t=TT)
        nxT = sb("nxT", [P, 2, KC, HF])
        cT = vst_mem[:, 0:2 * KC * HF].rearrange("p (h k t) -> p h k t", h=2, k=KC)
        stats = sb("stats", [P, 2, TT, 6])
        mv = sb("mv", [P, 2, TT, 2])
        veps = sb("veps", [P, 2, TT])
        rstd = sb("rstd", [P, 2, TT])
        parts = sb("parts", [P, 4, NPART, HF], BF16)
        rest = sb("rest", [P, 4, HF])
        vst = vst_mem[:, :].rearrange("p (a t h e) -> p a t h e", a=2, t=TT, h=H)
        cx = sb("cx", [KPX, 2, D])
        cxT = sb("cxT", [P, KC, LX])
        partsx = sb("partsx", [P, KC, NPART, LX], BF16)
        restx = sb("restx", [P, KC, LX])
        vstx = sb("vstx", [KPX, 2, H, NV])

        q_st = [sb(f"q_st{w}", [SROWS, 4, L], BF16) for w in range(4)]
        k_st = [sb(f"k_st{w}", [SROWS, 4, L], BF16) for w in range(4)]
        v_all = nx_mem[:, :].rearrange("p (c k e) -> p c k e", c=2, k=L // P)
        v_cur = [v_all[:, c] for c in range(2)]
        NPT = 8
        probs = sb("probs", [P, NPT, 2, HF])
        mx = sb("mx", [P, 2, 2, 32])
        mxc = sb("mxc", [P, 2, 32])
        nm = sb("nm", [32, 2, NPART, P], BF16)
        nmr = sb("nmr", [32, P])
        o_mem = [out_mem[:, 2 * HF * i:2 * HF * i + 2 * HF] for i in range(3)]
        oT = o_mem[0].rearrange("p (h c d) -> p h c d", h=2, d=32)
        rs = sb("rs", [P, 2, 16])
        oN = o_mem[1].rearrange("p (h c d) -> p h c d", h=2, d=32)
        oC = o_mem[2].rearrange("p (h t) -> p h t", h=2)
        hT = probs[:, :, :, :].rearrange("p a b t -> p (a b) t")[:, 0:FC, :]

        w_in = sem("w_in")
        w_late = sem("w_late")
        consts_ok = sem("consts_ok")
        pool_const = sem("pool_const")
        ones_ok = sem("ones_ok")

        class Dense:

            def __init__(self, n):
                self.x_in = [sem(f"{n}_x_in{i}") for i in range(2)]
                self.o_ready = sem(f"{n}_o_ready")
                self.xn_done = sem(f"{n}_xn_done")
                self.xn_stored = [sem(f"{n}_xn_stored{i}") for i in range(2)]
                self.stat_done, self.stat_seen = sem(f"{n}_stat_done"), sem(f"{n}_stat_seen")
                self.var_ready = sem(f"{n}_var_ready")
                self.eps_done = sem(f"{n}_eps_done")
                self.rstd_ready = sem(f"{n}_rstd_ready")
                self.nx_ready = sem(f"{n}_nx_ready")
                self.tp_ready = sem(f"{n}_tp_ready")
                self.nxT_ready = sem(f"{n}_nxT_ready")
                self.p_ready = sem(f"{n}_p_ready")
                self.hi_ready = sem(f"{n}_hi_ready")
                self.rest_ready, self.rest_seen = sem(f"{n}_rest_ready"), sem(f"{n}_rest_seen")
                self.mid_done = sem(f"{n}_mid_done")
                self.parts_ready = sem(f"{n}_parts_ready")
                self.parts_stored = [sem(f"{n}_parts_stored{i}") for i in range(4)]

        A, C, E = Dense("A"), Dense("C"), Dense("E")
        v_ready, v_evac = sem("v_ready"), sem("v_evac")
        v_stored = [sem(f"v_stored{i}") for i in range(2)]
        cx_in, ctp_ready, cxT_ready = sem("cx_in"), sem("ctp_ready"), sem("cxT_ready")
        px_stored = [sem(f"px_stored{i}") for i in range(2)]
        vx_stored = sem("vx_stored")
        h_ready, h_evac = sem("h_ready"), sem("h_evac")
        xb_ready = sem("xb_ready")
        f_ready, y_done = sem("f_ready"), sem("y_done")
        y_stored = [sem(f"y_stored{i}") for i in range(2)]

        class Attention:

            def __init__(self, n, causal, kp, nkb, qp, kp_dram, v_dram, out_dram):
                self.causal, self.kp, self.nkb, self.nk = causal, kp, nkb, kp * nkb
                self.q_dram, self.k_dram, self.v_dram, self.out_dram = qp, kp_dram, v_dram, out_dram
                self.steps = []
                for hf in range(2):
                    for kb in range(4 * (hf + 1) if causal else nkb):
                        lo = max(HF * hf, P * kb) if causal else HF * hf
                        self.steps.append((hf, kb, lo, HF * (hf + 1) - lo))
                self.NS = len(self.steps)
                self.tiles = []
                for i in range(4):
                    if causal:
                        for qb in range(8):
                            n_keys = P * (qb + 1)
                            self.tiles.append((i, qb, 1, 0, min(n_keys, HF), 0))
                            if n_keys > HF:
                                self.tiles.append((i, qb, 1, HF, n_keys - HF, 1))
                    else:
                        self.tiles += [(i, 0, 3, 0, self.nk, 0), (i, 3, 3, 0, self.nk, 0), (i, 6, 2, 0, self.nk, 0)]
                self.MT = len(self.tiles)
                self.TPS = self.MT // self.NS
                self.last = [max(s for s in range(self.NS) if self.steps[s][0] == hf) for hf in range(2)]
                self.diag = [s for s in range(self.NS) if causal and P * self.steps[s][1] >= HF * self.steps[s][0]]
                self.ND = 2 * len(self.diag)
                self.stack_in = [sem(f"{n}_stack_in{w}") for w in range(4)]
                self.v_in = [sem(f"{n}_v_in{c}") for c in range(2)]
                self.m_ready = sem(f"{n}_m_ready")
                self.m_free = sem(f"{n}_m_free")
                self.mxc_ready = sem(f"{n}_mxc_ready")
                self.nm_hi = sem(f"{n}_nm_hi")
                self.nm_mid = sem(f"{n}_nm_mid")
                self.nm_ready = sem(f"{n}_nm_ready")
                self.rows_out = [sem(f"{n}_rows_out{i}") for i in range(2)]
                self.rows_in = [sem(f"{n}_rows_in{i}") for i in range(2)]
                self.st_ready = sem(f"{n}_st_ready")
                self.exp_done, self.exp_seen = sem(f"{n}_exp_done"), sem(f"{n}_exp_seen")
                self.mask_done = sem(f"{n}_mask_done")
                self.pv_done = sem(f"{n}_pv_done")
                self.acc_free = sem(f"{n}_acc_free")
                self.rs_done = sem(f"{n}_rs_done")
                self.oN_done = sem(f"{n}_oN_done")
                self.oC_ready = [sem(f"{n}_oC_ready{i}") for i in range(2)]
                self.oC_stored = [sem(f"{n}_oC_stored{i}") for i in range(2)]

            def tile_use(self, v, n):
                if isinstance(v, int) and v == 0:
                    return n
                return (self.MT + 1) * v + n - (n < self.TPS)

            def turn_use(self, v):
                return (self.MT + 1) * (v + 1) - 1 + self.TPS * (v < 4 * B - 1)

        SA = Attention("S", True, P, L // P, q_parts, k_parts, v_aug, self_ctx)
        XA = Attention("X", False, KPX, 2, qx_parts, kx_parts, vx_aug, cross_ctx)

        LAG = 2
        PROBS_STEPS = NPT // 2

        def sequence(eng, a, slot):
            per = 4 * a.NS
            for q in range(LAG):
                slot(q, 0)
            with eng.Fori(0, B - 1) as b:
                for q in range(LAG, LAG + per):
                    slot(q, b)
            for q in range(LAG + (B - 1) * per, B * per + LAG):
                slot(q, 0)

        block = ctx.enter_context(nc.Block())

        @block.sync
        def _(sp):
            def load_x(ph, src, b, hf):
                sp.dma_start(xt[:, hf], tokens(src, b, hf)).then_inc(ph.x_in[hf], 16)

            def load_ctx(b):
                sp.dma_start(cx[:, :, :], one(ctx_in, b).rearrange("b (k p) d -> p (b k) d", p=KPX)).then_inc(cx_in, 16)

            for s in range(4):
                sp.sem_inc(A.parts_stored[s], 16)
            for s in range(2):
                sp.sem_inc(v_stored[s], 16)
                sp.sem_inc(px_stored[s], 16)
            sp.sem_inc(vx_stored, 16)
            for hf in range(2):
                load_x(A, x, 0, hf)
            load_ctx(0)

            def store_a(b, more):
                if more:
                    for hf in range(2):
                        sp.wait_ge(A.nx_ready, 2 * b + hf + 1)
                        load_x(A, x, b + 1, hf)
                for hf in range(2):
                    for s in range(4):
                        dst = (q_parts, k_parts)[s // 2]
                        sp.wait_ge(A.parts_ready, 10 * b + 4 * hf + s + 1)
                        sp.dma_start(one(dst, 2 * b + s % 2).rearrange("u s p t -> p (u s) t")[:, :, HF * hf:HF * hf + HF],
                                     parts[:, s]).then_inc(A.parts_stored[s], 16)
                    sp.wait_ge(v_evac, 2 + 5 * b + 2 * hf + 2)
                    sp.dma_start(tokens(v_aug, b, hf),
                                 vst[:, hf].rearrange("p t h e -> p t (h e)")).then_inc(v_stored[hf], 16)
                if more:
                    sp.wait_ge(ctp_ready, b + 1)
                    load_ctx(b + 1)
                for c in range(2):
                    sp.wait_ge(A.parts_ready, 10 * b + 8 + c + 1)
                    sp.dma_start(one(kx_parts, 2 * b + c).rearrange("u s p t -> p (u s) t"),
                                 partsx[:, c]).then_inc(px_stored[c], 16)
                sp.wait_ge(v_evac, 2 + 5 * b + 5)
                sp.dma_start(one(vx_aug, b).rearrange("b (k p) e -> p (b k) e", p=KPX),
                             vstx[:, :].rearrange("p k h e -> p k (h e)")).then_inc(vx_stored, 16)

            with sp.Fori(0, B - 1) as b:
                store_a(b, True)
            store_a(B - 1, False)
            for s in range(4):
                sp.wait_ge(A.parts_stored[s], 16 + 16 * 2 * B)
            for s in range(2):
                sp.wait_ge(v_stored[s], 16 + 16 * B)
                sp.wait_ge(px_stored[s], 16 + 16 * B)
            sp.wait_ge(vx_stored, 16 + 16 * B)

            def attention(a):
                def load(v0, b):
                    w, u = v0 % 4, v0 // 2 + 2 * b
                    for s in range(NPROD):
                        for st, src, part, n in ((q_st, a.q_dram, Q_PARTS[s], L), (k_st, a.k_dram, K_PARTS[s], a.nk)):
                            sp.dma_start(st[w][DK * s:DK * s + DK, :, 0:n],
                                         one(src, u).rearrange("u s (i g d) t -> d (u s) g i t", g=2, d=DK)[:, part, w % 2]
                                         ).then_inc(a.stack_in[w], 16)
                    if w % 2:
                        sp.dma_start(v_cur[w // 2][0:a.kp, 0:a.nkb, :],
                                     one(a.v_dram, v0 // 4 + b).rearrange("b (k p) (c e) -> p (b k) c e", p=a.kp, c=2)[:, :, w // 2]
                                     ).then_inc(a.v_in[w // 2], 16)

                def rows(v0, b):
                    v, par = v0 + 4 * b, v0 % 2
                    sp.wait_ge(a.nm_ready, v + 1)
                    sp.dma_start(max_rows[par].rearrange("s r t -> r s t"), nm[:, par]).then_inc(a.rows_out[par], 16)
                    sp.wait_ge(a.rows_out[par], 16 * (v0 // 2 + 2 * b + 1))
                    sp.dma_start(q_st[v0 % 4][KROWS:SROWS, :, :],
                                 max_rows[par].rearrange("s (i q) t -> s i (q t)", i=4)).then_inc(a.rows_in[par], 16)

                def store(v0, b, hf):
                    u = v0 // 2 + 2 * b
                    sp.wait_ge(a.oC_ready[hf], u + 1)
                    sp.dma_start(one(a.out_dram, u).rearrange("u p t -> p (u t)")[:, HF * hf:HF * hf + HF],
                                 oC[:, hf]).then_inc(a.oC_stored[hf], 16)

                def window(v0, b):
                    v = v0 + 4 * b
                    if v0 + 1 < 4 * B:
                        rows(v0 + 1, b)
                    if v0 + 3 < 4 * B:
                        sp.wait_ge(a.pv_done, PROBS_STEPS + a.NS * v)
                        load(v0 + 3, b)
                    if v0 % 2:
                        store(v0, b, 0)
                        store(v0, b, 1)

                for hf in range(2):
                    sp.sem_inc(a.oC_stored[hf], 16)
                for v in range(3):
                    load(v, 0)
                rows(0, 0)
                with sp.Fori(0, B - 1) as b:
                    for w in range(4):
                        window(w, b)
                for w in range(4):
                    window(4 * (B - 1) + w, 0)
                for hf in range(2):
                    sp.wait_ge(a.oC_stored[hf], 16 + 16 * 2 * B)

            attention(SA)

            def load_dense(ph, src, cdram, b, hf):
                load_x(ph, src, b, hf)
                sp.dma_start(cT[:, hf], cdram[bass.ds(2 * b, 2)].rearrange("c p t -> p c t")[:, :, HF * hf:HF * hf + HF]
                             ).then_inc(ph.x_in[hf], 16)

            for s in range(2):
                sp.sem_inc(C.parts_stored[s], 16)
                sp.sem_inc(C.xn_stored[s], 16)
            for hf in range(2):
                load_dense(C, x, self_ctx, 0, hf)

            def store_c(b, more):
                for hf in range(2):
                    n = 2 * b + hf
                    sp.wait_ge(C.xn_done, 2 + 2 * n + 2)
                    sp.dma_start(tokens(x1_dram, b, hf), xn[:, hf]).then_inc(C.xn_stored[hf], 16)
                    if more:
                        load_dense(C, x, self_ctx, b + 1, hf)
                    for c in range(2):
                        sp.wait_ge(C.parts_ready, 2 * n + c + 1)
                        sp.dma_start(one(qx_parts, 2 * b + c).rearrange("u s p t -> p (u s) t")[:, :, HF * hf:HF * hf + HF],
                                     parts[:, c]).then_inc(C.parts_stored[c], 16)

            with sp.Fori(0, B - 1) as b:
                store_c(b, True)
            store_c(B - 1, False)
            for s in range(2):
                sp.wait_ge(C.parts_stored[s], 16 + 16 * 2 * B)
                sp.wait_ge(C.xn_stored[s], 16 + 16 * B)

            attention(XA)

            for hf in range(2):
                sp.sem_inc(y_stored[hf], 16)
                load_dense(E, x1_dram, cross_ctx, 0, hf)

            def store_e(b, more):
                for hf in range(2):
                    n = 2 * b + hf
                    sp.wait_ge(y_done, 2 + 2 * n + 2)
                    sp.dma_start(tokens(out, b, hf), xn[:, hf]).then_inc(y_stored[hf], 16)
                    if more:
                        load_dense(E, x1_dram, cross_ctx, b + 1, hf)

            with sp.Fori(0, B - 1) as b:
                store_e(b, True)
            store_e(B - 1, False)
            for hf in range(2):
                sp.wait_ge(y_stored[hf], 16 + 16 * B)

        @block.tensor
        def _(pe):
            def transposes(ph, n, hf, b0):
                pe.wait_ge(ph.nx_ready, n + 1)
                for k in range(KC):
                    for t in range(TT):
                        last = pe.transpose(bank[:, b0 + k, P * t:P * t + P], nx[:, hf, t, P * k:P * k + P], ident[:, :])
                    last.then_inc(ph.tp_ready, 1)

            def project(dst, w, cols, src):
                for k in range(KC):
                    last = pe.matmul(dst, w[:, k, cols], src[:, k, :], start=(k == 0), stop=(k == KC - 1))
                return last

            pe.wait_ge(w_in, 16 * 9)
            pe.wait_ge(consts_ok, 3)

            def dense_a(b):
                for hf in range(2):
                    n = 2 * b + hf
                    transposes(A, n, hf, 0)
                    pe.wait_ge(A.nxT_ready, 2 * n + 2)
                    for s in range(4):
                        before = 10 * b + s if hf else 10 * b - 10 + (8 if s < 2 else 4) + s
                        pe.wait_ge(A.rest_ready, 10 + before + 1)
                        project(bank[:, 2 + s], wqkv_sb, slice(P * s, P * s + P), nxT[:, hf]).then_inc(A.p_ready, 1)
                    for i in range(2):
                        pe.wait_ge(v_evac, 2 + 5 * b + ((0, -1), (1, 2))[hf][i])
                        for t in range(2 * i, 2 * i + 2):
                            for k in range(KC):
                                last = pe.matmul(bank[:, 6 + i, D * (t % 2):D * (t % 2) + D], nxT[:, hf, k, P * t:P * t + P],
                                                 wqkv_sb[:, k, 2 * D:3 * D], start=(k == 0), stop=(k == KC - 1))
                        last.then_inc(v_ready, 1)
                pe.wait_ge(cx_in, 16 * b + 16)
                for k in range(KC):
                    for kb in range(2):
                        last = pe.transpose(bank[:, 0, LX * k + KPX * kb:LX * k + KPX * kb + KPX], cx[:, kb, P * k:P * k + P],
                                            ident[0:KPX, 0:KPX])
                last.then_inc(ctp_ready, 1)
                pe.wait_ge(cxT_ready, b + 1)
                for c in range(2):
                    pe.wait_ge(A.rest_ready, 10 + 10 * b + 4 + c + 1)
                    project(bank[:, 2 + c, 0:LX], wkv_sb, slice(P * c, P * c + P), cxT).then_inc(A.p_ready, 1)
                pe.wait_ge(v_evac, 2 + 5 * b + 3)
                for kb in range(2):
                    for k in range(KC):
                        last = pe.matmul(bank[0:KPX, 6, D * kb:D * kb + D], cxT[:, k, KPX * kb:KPX * kb + KPX],
                                         wkv_sb[:, k, D:2 * D], start=(k == 0), stop=(k == KC - 1))
                last.then_inc(v_ready, 1)

            with pe.Fori(0, B) as b:
                dense_a(b)

            def attention(a):
                pe.sem_inc(a.pv_done, PROBS_STEPS)

                def max_tile(v0, b, n):
                    v, w = v0 + 4 * b, v0 % 4
                    i, qb, nq, k0, keys, _ = a.tiles[n]
                    use, slot = a.tile_use(v, n), a.tile_use(v0, n) % 2
                    if n == 0:
                        pe.wait_ge(a.stack_in[w], 16 * 2 * NPROD * (v0 // 4 + b + 1))
                    if v0 or n >= 2:
                        pe.wait_ge(a.m_free, use - 1)
                    masked = a.causal and k0 + keys == P * (qb + 1)
                    for j in range(nq):
                        last = pe.matmul(bank[:, 6 + slot, keys * j:keys * j + keys],
                                         q_st[w][0:KROWS, i, P * (qb + j):P * (qb + j) + P],
                                         k_st[w][0:KROWS, i, k0:k0 + keys], start=True, stop=not masked)
                    if masked:
                        last = pe.matmul(bank[:, 6 + slot, keys - P:keys], ident_bf[:, :], causal_bf[:, :], start=False, stop=True)
                    last.then_inc(a.m_ready, 1)

                def turn(v0, b):
                    v, par = v0 + 4 * b, v0 % 2
                    use, slot = a.turn_use(v0) + 4 * b * (a.MT + 1), a.turn_use(v0) % 2
                    if a.causal:
                        pe.wait_ge(a.mxc_ready, v + 1)
                    pe.wait_ge(a.m_free, use - (v0 < 4 * B - 1))
                    src = mxc[:, par] if a.causal else mx[:, par, 0]
                    pe.transpose(bank[0:32, 6 + slot, 0:P], src, ident[:, :]).then_inc(a.m_ready, 1)

                def stream(v0, b, s, some):
                    if v0 < 4 * B:
                        for n in some:
                            max_tile(v0, b, a.TPS * s + n)
                    if s == 0 and some[-1] == a.TPS - 1 and 1 <= v0 <= 4 * B:
                        turn(v0 - 1, b)

                def scores(v0, b, s, p):
                    v, w = v0 + 4 * b, v0 % 4
                    hf, kb, lo, n = a.steps[s]
                    use = 2 * (a.NS * v + s) + p
                    if s == 0:
                        pe.wait_ge(a.rows_in[v0 % 2], 16 * (v0 // 2 + 2 * b + 1))
                    pe.wait_ge(a.exp_done, 2 + use - 1)
                    for j in range(2):
                        last = pe.matmul(bank[0:a.kp, 2 * p + j, 0:n], k_st[w][:, 2 * p + j, a.kp * kb:a.kp * kb + a.kp],
                                         q_st[w][:, 2 * p + j, lo:lo + n], start=True, stop=True)
                    last.then_inc(a.st_ready, 1)

                def weigh(v0, b, s):
                    v, w = v0 + 4 * b, v0 % 4
                    hf, kb, lo, n = a.steps[s]
                    if s == 0 and w % 2 == 0:
                        pe.wait_ge(a.v_in[w // 2], 16 * (v0 // 4 + b + 1))
                    if kb == 0:
                        pe.wait_ge(a.acc_free, 2 + 2 * v + hf - 1)
                    if s in a.diag:
                        pe.wait_ge(a.mask_done, a.ND * v + 2 * a.diag.index(s) + 2)
                    else:
                        pe.wait_ge(a.exp_done, 2 + 2 * (a.NS * v + s) + 2)
                    for i in range(4):
                        pt = (2 * (a.NS * v0 + s) + i // 2) % NPT
                        last = pe.matmul(bank[32 * i:32 * i + NV, 4 + hf, lo - HF * hf:lo - HF * hf + n],
                                         v_cur[w // 2][0:a.kp, kb, NV * (2 * i + w % 2):NV * (2 * i + w % 2) + NV],
                                         probs[0:a.kp, pt, i % 2, 0:n], start=(kb == 0), stop=(s == a.last[hf]))
                    last.then_inc(a.pv_done, 1)

                def slot(q, b):
                    v0, s = q // a.NS, q % a.NS
                    live = v0 < 4 * B
                    if live:
                        scores(v0, b, s, 0)
                    stream(v0 + 2, b, s, [0])
                    if live:
                        scores(v0, b, s, 1)
                    stream(v0 + 2, b, s, [1])
                    if q >= LAG:
                        weigh((q - LAG) // a.NS, b, (q - LAG) % a.NS)
                    stream(v0 + 2, b, s, range(2, a.TPS))

                for v in range(2):
                    for s in range(a.NS):
                        stream(v, 0, s, range(a.TPS))
                sequence(pe, a, slot)

            pe.wait_ge(v_evac, 2 + 5 * B)
            pe.wait_ge(A.rest_ready, 10 + 10 * B)
            pe.wait_ge(ones_ok, 5)
            attention(SA)

            def out_project(ph, w, b, hf):
                n = 2 * b + hf
                pe.wait_ge(ph.x_in[hf], 32 * b + 32)
                for i in range(2):
                    pe.wait_ge(ph.xn_done, 2 + 2 * n + i - 1)
                    for t in range(2 * i, 2 * i + 2):
                        for k in range(KC):
                            last = pe.matmul(bank[:, i, D * (t % 2):D * (t % 2) + D], cT[:, hf, k, P * t:P * t + P], w[:, k, :],
                                             start=(k == 0), stop=(k == KC - 1))
                    last.then_inc(ph.o_ready, 1)

            def dense_c(b, more):
                for hf in range(2):
                    n = 2 * b + hf
                    if hf == 0:
                        out_project(C, wso_sb, b, 1)
                    elif more:
                        out_project(C, wso_sb, b + 1, 0)
                    transposes(C, n, hf, 2)
                    pe.wait_ge(C.nxT_ready, 2 * n + 2)
                    for c in range(2):
                        pe.wait_ge(C.rest_ready, 2 + 2 * n + c - 1)
                        project(bank[:, 4 + c], wq_sb, slice(P * c, P * c + P), nxT[:, hf]).then_inc(C.p_ready, 1)

            pe.wait_ge(SA.acc_free, 2 + 2 * 4 * B)
            pe.wait_ge(SA.exp_done, 2 + 2 * 4 * B * SA.NS)
            pe.wait_ge(w_late, 16 * 6)
            out_project(C, wso_sb, 0, 0)
            with pe.Fori(0, B - 1) as b:
                dense_c(b, True)
            dense_c(B - 1, False)

            pe.wait_ge(C.rest_ready, 2 + 2 * 2 * B)
            attention(XA)

            def dense_e(b, more):
                for hf in range(2):
                    n = 2 * b + hf
                    if hf == 0:
                        out_project(E, wco_sb, b, 1)
                    elif more:
                        out_project(E, wco_sb, b + 1, 0)
                    transposes(E, n, hf, 2)
                    pe.wait_ge(E.nxT_ready, 2 * n + 2)
                    for f in range(FC):
                        pe.wait_ge(h_evac, 2 + FC * n + f - 1)
                        project(bank[:, 4 + f % 2], w1_sb, slice(P * f, P * f + P), nxT[:, hf]).then_inc(h_ready, 1)
                    pe.wait_ge(h_evac, 2 + FC * n + FC)
                    for i in range(2):
                        pe.wait_ge(y_done, 2 + 2 * n + i - 1)
                        for t in range(2 * i, 2 * i + 2):
                            for f in range(FC):
                                last = pe.matmul(bank[:, 6 + i, D * (t % 2):D * (t % 2) + D], hT[:, f, P * t:P * t + P],
                                                 w2_sb[:, f, :], start=(f == 0), stop=(f == FC - 1))
                        last.then_inc(f_ready, 1)

            pe.wait_ge(XA.acc_free, 2 + 2 * 4 * B)
            pe.wait_ge(XA.exp_done, 2 + 2 * 4 * B * XA.NS)
            out_project(E, wco_sb, 0, 0)
            with pe.Fori(0, B - 1) as b:
                dense_e(b, True)
            dense_e(B - 1, False)

        @block.scalar
        def _(act):
            act.dma_start(wqkv_sb[:, :, :], w_qkv.rearrange("(k p) n -> p k n", p=P)).then_inc(w_in, 16)
            act.dma_start(wkv_sb[:, :, :], w_kv.rearrange("(k p) n -> p k n", p=P)).then_inc(w_in, 16)
            with nc.allow_non_contiguous_dma(reason="vectors of 256 and 1024 elements"):
                for i, (s, z) in enumerate(((ln1_s, ln1_b), (ln2_s, ln2_b), (ln3_s, ln3_b))):
                    act.dma_start(lns_sb[:, i, :], s.rearrange("(k p) -> p k", p=P)).then_inc(w_in, 16)
                    act.dma_start(lnb_sb[:, i, :], z.rearrange("(k p) -> p k", p=P)).then_inc(w_in, 16)
                act.dma_start(b1_sb[:, :], b1.rearrange("(k p) -> p k", p=P)).then_inc(w_in, 16)
            act.dma_start(b2_sb[:, :], b2.partition_broadcast(P)).then_inc(w_late, 16)
            for dst, src in ((wso_sb, w_self_out), (wq_sb, w_q), (wco_sb, w_cross_out), (w1_sb, w1), (w2_sb, w2)):
                act.dma_start(dst[:, :, :], src.rearrange("(k p) n -> p k n", p=P)).then_inc(w_late, 16)

            act.sem_inc(v_evac, 2)
            act.sem_inc(h_evac, 2)
            act.sem_inc(SA.exp_done, 2)
            act.sem_inc(XA.exp_done, 2)

            def scaled(ph, i, n, hf, b0):
                for k in range(KC):
                    act.wait_ge(ph.tp_ready, 2 * n + k + 1)
                    act.activation(nxT[:, hf, k, :], bank[:, b0 + k, :], ACT.Identity, bias=lnb_sb[:, i, k:k + 1],
                                   scale=lns_sb[:, i, k:k + 1]).then_inc(ph.nxT_ready, 1)

            act.wait_ge(w_in, 16 * 9)
            act.wait_ge(ones_ok, 5)

            with act.Fori(0, B) as b:
                for hf in range(2):
                    n = 2 * b + hf
                    scaled(A, 0, n, hf, 0)
                    for s in range(4):
                        act.wait_ge(A.p_ready, 10 * b + 4 * hf + s + 1)
                        act.wait_ge(A.parts_stored[s], 16 * n + 16)
                        act.copy(parts[:, s, 0, :], bank[:, 2 + s, :]).then_inc(A.hi_ready, 1)
                    act.wait_ge(v_stored[hf], 16 * b + 16)
                    for i in range(2):
                        act.wait_ge(v_ready, 5 * b + 2 * hf + i + 1)
                        for t in range(2 * i, 2 * i + 2):
                            last = act.copy(vst[:, hf, t, :, 0:DK],
                                            bank[:, 6 + i, D * (t % 2):D * (t % 2) + D].rearrange("p (h d) -> p h d", d=DK))
                        last.then_inc(v_evac, 1)
                act.wait_ge(ctp_ready, b + 1)
                act.copy(cxT[:, :, :], bank[:, 0, 0:KC * LX].rearrange("p (k t) -> p k t", k=KC)).then_inc(cxT_ready, 1)
                for c in range(2):
                    act.wait_ge(A.p_ready, 10 * b + 8 + c + 1)
                    act.wait_ge(px_stored[c], 16 * b + 16)
                    act.copy(partsx[:, c, 0, :], bank[:, 2 + c, 0:LX]).then_inc(A.hi_ready, 1)
                act.wait_ge(vx_stored, 16 * b + 16)
                act.wait_ge(v_ready, 5 * b + 5)
                for kb in range(2):
                    last = act.copy(vstx[:, kb, :, 0:DK], bank[0:KPX, 6, D * kb:D * kb + D].rearrange("p (h d) -> p h d", d=DK))
                last.then_inc(v_evac, 1)

            def attention(a):
                def slot(q, b):
                    v0, s = q // a.NS, q % a.NS
                    if v0 >= 4 * B:
                        return
                    v = v0 + 4 * b
                    n = a.steps[s][3]
                    step = a.NS * v + s
                    act.wait_ge(a.pv_done, step + 1)
                    for p in range(2):
                        act.wait_ge(a.st_ready, 2 * step + p + 1)
                        pt = (2 * (a.NS * v0 + s) + p) % NPT
                        act.activation(probs[0:a.kp, pt, :, 0:n], bank[0:a.kp, 2 * p:2 * p + 2, 0:n], ACT.Exp,
                                       scale=SCALE).then_inc(a.exp_done, 1)

                sequence(act, a, slot)

            attention(SA)

            with act.Fori(0, B) as b:
                for hf in range(2):
                    n = 2 * b + hf
                    scaled(C, 1, n, hf, 2)
                    for c in range(2):
                        act.wait_ge(C.p_ready, 2 * n + c + 1)
                        act.wait_ge(C.parts_stored[c], 16 * n + 16)
                        act.copy(parts[:, c, 0, :], bank[:, 4 + c, :]).then_inc(C.hi_ready, 1)

            attention(XA)

            with act.Fori(0, B) as b:
                for hf in range(2):
                    n = 2 * b + hf
                    scaled(E, 2, n, hf, 2)
                    for f in range(FC):
                        act.wait_ge(h_ready, FC * n + f + 1)
                        act.activation(hT[:, f, :], bank[:, 4 + f % 2, :], ACT.Relu, bias=b1_sb[:, f:f + 1]).then_inc(h_evac, 1)

        @block.vector
        def _(dve):
            for w in range(4):
                last = dve.memset(k_st[w][KROWS:SROWS, :, :], 1.0)
            last.then_inc(ones_ok, 1)
            dve.memset(vst[:, :, :, :, DK:NV].rearrange("p a t h e -> p (a t h) e"), 1.0).then_inc(ones_ok, 1)
            dve.memset(vstx[:, :, :, DK:NV].rearrange("p k h e -> p (k h) e"), 1.0).then_inc(ones_ok, 1)
            dve.memset(mx[:, :, :, :].rearrange("p a b c -> p (a b c)"), LOWEST).then_inc(ones_ok, 1)
            dve.memset(bank[:, 4:6, :], 0.0).then_inc(ones_ok, 1)

            for ph, k in ((A, 10), (C, 2)):
                dve.sem_inc(ph.rest_ready, k)
            for ph in (C, E):
                dve.sem_inc(ph.xn_done, 2)
            dve.sem_inc(y_done, 2)
            for a in (SA, XA):
                dve.sem_inc(a.acc_free, 2)

            def moments(ph, src, n, hf):
                for t in range(TT):
                    last = dve.bn_stats(stats[:, hf, t, :], src[:, hf, t, :])
                last.then_inc(ph.stat_done, 1)
                dve.wait_ge(ph.stat_done, n + 1)
                dve.sem_inc(ph.stat_seen, 1)
                for t in range(TT):
                    last = dve.bn_aggr(mv[:, hf, t, :], stats[:, hf, t, :])
                last.then_inc(ph.var_ready, 1)

            def normalize(ph, src, n, hf):
                dve.wait_ge(ph.rstd_ready, n + 1)
                for t in range(TT):
                    last = dve.tensor_scalar(nx[:, hf, t, :], src[:, hf, t, :], mv[:, hf, t, 0:1], rstd[:, hf, t:t + 1],
                                             ALU.subtract, ALU.mult)
                last.then_inc(ph.nx_ready, 1)

            def split(ph, use, dst, src, hi):
                dve.wait_ge(ph.hi_ready, use + 1)
                dve.tensor_tensor(dst, src, hi, ALU.subtract).then_inc(ph.rest_ready, 1)

            def norm_a(b, hf):
                dve.wait_ge(A.x_in[hf], 16 * b + 16)
                moments(A, xt, 2 * b + hf, hf)
                normalize(A, xt, 2 * b + hf, hf)

            def dense_a(b, more):
                for hf in range(2):
                    for s in range(4):
                        split(A, 10 * b + 4 * hf + s, rest[:, s], bank[:, 2 + s, :], parts[:, s, 0, :])
                    if more:
                        norm_a(b + 1, hf)
                for c in range(2):
                    split(A, 10 * b + 8 + c, restx[:, c], bank[:, 2 + c, 0:LX], partsx[:, c, 0, :])

            for hf in range(2):
                norm_a(0, hf)
            with dve.Fori(0, B - 1) as b:
                dense_a(b, True)
            dense_a(B - 1, False)

            def attention(a):
                def max_tile(v0, b, n):
                    v, par = v0 + 4 * b, v0 % 2
                    i, qb, nq, _, keys, part = a.tiles[n]
                    use, slot = a.tile_use(v, n), a.tile_use(v0, n) % 2
                    dve.wait_ge(a.m_ready, use + 1)
                    dve.tensor_reduce(mx[:, par, part, 8 * i + qb:8 * i + qb + nq],
                                      bank[:, 6 + slot, 0:nq * keys].rearrange("p (q k) -> p q k", q=nq), AX.X, ALU.max
                                      ).then_inc(a.m_free, 1)
                    if a.causal and n == a.MT - 1:
                        dve.wait_ge(a.m_free, use + 1)
                        dve.tensor_tensor(mxc[:, par], mx[:, par, 0], mx[:, par, 1], ALU.max).then_inc(a.mxc_ready, 1)

                def negate(v0, b):
                    v, par = v0 + 4 * b, v0 % 2
                    use, slot = a.turn_use(v0) + 4 * b * (a.MT + 1), a.turn_use(v0) % 2
                    src = bank[0:32, 6 + slot, 0:P]
                    if v0 >= 2:
                        dve.wait_ge(a.rows_in[par], 16 * (v0 // 2 + 2 * b))
                    dve.wait_ge(a.m_ready, use + 1)
                    dve.tensor_scalar(nm[:, par, 0, :], src, -1.0, None, ALU.mult).then_inc(a.nm_hi, 1)
                    dve.wait_ge(a.nm_hi, v + 1)
                    dve.scalar_tensor_tensor(out=nmr[:, :], in0=src, scalar=-1.0, in1=nm[:, par, 0, :], op0=ALU.mult,
                                             op1=ALU.subtract).then_inc(a.m_free, 1)
                    dve.wait_ge(a.m_free, use + 1)
                    dve.tensor_copy(nm[:, par, 1, :], nmr[:, :]).then_inc(a.nm_mid, 1)
                    dve.wait_ge(a.nm_mid, v + 1)
                    dve.tensor_tensor(nm[:, par, 2, :], nmr[:, :], nm[:, par, 1, :], ALU.subtract).then_inc(a.nm_ready, 1)

                def finish(v0, b, hf):
                    v, g = v0 + 4 * b, v0 % 2
                    u = v0 // 2 + 2 * b
                    dve.wait_ge(a.pv_done, PROBS_STEPS + a.NS * v + a.last[hf] + 1)
                    dve.transpose(oT[:, hf].rearrange("p c d -> p (c d)"), bank[:, 4 + hf, :]).then_inc(a.acc_free, 1)
                    dve.wait_ge(a.acc_free, 2 + 2 * v + hf + 1)
                    dve.reciprocal(rs[:, hf, :], oT[:, hf, :, DK]).then_inc(a.rs_done, 1)
                    dve.wait_ge(a.rs_done, 2 * v + hf + 1)
                    dve.tensor_tensor(oN[:, hf, :, DK * g:DK * g + DK], oT[:, hf, :, 0:DK],
                                      rs[:, hf, :].unsqueeze(2).to_broadcast([P, 16, DK]), ALU.mult).then_inc(a.oN_done, 1)
                    if g:
                        dve.wait_ge(a.oN_done, 2 * v + hf + 1)
                        dve.wait_ge(a.oC_stored[hf], 16 * u + 16)
                        dve.transpose(oC[:, hf, :], oN[:, hf].rearrange("p c d -> p (c d)")).then_inc(a.oC_ready[hf], 1)

                def stream(v0, b, s):
                    if v0 < 4 * B:
                        for n in range(a.TPS):
                            max_tile(v0, b, a.TPS * s + n)
                    if s == 0 and 1 <= v0 <= 4 * B:
                        negate(v0 - 1, b)

                def slot(q, b):
                    v0, s = q // a.NS, q % a.NS
                    stream(v0 + 2, b, s)
                    done = q - LAG
                    for hf in range(2):
                        if done >= 0 and done % a.NS == a.last[hf]:
                            finish(done // a.NS, b, hf)

                for v in range(2):
                    for s in range(a.NS):
                        stream(v, 0, s)
                sequence(dve, a, slot)

            attention(SA)

            def residual(ph, b, hf):
                n = 2 * b + hf
                dve.wait_ge(ph.x_in[hf], 32 * b + 32)
                for i in range(2):
                    dve.wait_ge(ph.o_ready, 2 * n + i + 1)
                    dve.tensor_tensor(xn[:, hf, 2 * i:2 * i + 2, :], xt[:, hf, 2 * i:2 * i + 2, :],
                                      bank[:, i, :].rearrange("p (t d) -> p t d", t=2), ALU.add).then_inc(ph.xn_done, 1)
                dve.wait_ge(ph.xn_done, 2 + 2 * n + 2)
                moments(ph, xn, n, hf)

            def ahead_c(b, hf):
                dve.wait_ge(C.xn_stored[hf], 16 * b + 16)
                residual(C, b, hf)

            def dense_c(b, more):
                for hf in range(2):
                    n = 2 * b + hf
                    normalize(C, xn, n, hf)
                    if hf == 0:
                        ahead_c(b, 1)
                    elif more:
                        ahead_c(b + 1, 0)
                    for c in range(2):
                        split(C, 2 * n + c, rest[:, c], bank[:, 4 + c, :], parts[:, c, 0, :])

            ahead_c(0, 0)
            with dve.Fori(0, B - 1) as b:
                dense_c(b, True)
            dense_c(B - 1, False)

            attention(XA)

            def ahead_e(b, hf):
                dve.wait_ge(y_stored[hf], 16 * b + 16)
                residual(E, b, hf)

            def dense_e(b, more):
                for hf in range(2):
                    n = 2 * b + hf
                    normalize(E, xn, n, hf)
                    if hf == 0:
                        ahead_e(b, 1)
                    elif more:
                        ahead_e(b + 1, 0)
                    dve.wait_ge(xb_ready, n + 1)
                    for i in range(2):
                        dve.wait_ge(f_ready, 2 * n + i + 1)
                        dve.tensor_tensor(xn[:, hf, 2 * i:2 * i + 2, :], xt[:, hf, 2 * i:2 * i + 2, :],
                                          bank[:, 6 + i, :].rearrange("p (t d) -> p t d", t=2), ALU.add).then_inc(y_done, 1)

            ahead_e(0, 0)
            with dve.Fori(0, B - 1) as b:
                dense_e(b, True)
            dense_e(B - 1, False)

        @block.gpsimd
        def _(pool):
            pool.memset(ident[:, :], 0.0).then_inc(pool_const, 1)
            pool.memset(ident_bf[:, :], 0.0).then_inc(pool_const, 1)
            pool.memset(causal_bf[:, :], 0.0).then_inc(pool_const, 1)
            pool.memset(minus_half[:, :], -0.5).then_inc(pool_const, 1)
            pool.memset(eps_sb[:, :], EPS).then_inc(pool_const, 1)
            pool.wait_ge(pool_const, 5)
            for t in (ident, ident_bf):
                pool.affine_select(out=t[:, :], in_=t[:, :], compare_op=ALU.not_equal, fill=1.0, base=0,
                                   pattern=[[1, P]], channel_multiplier=-1).then_inc(consts_ok, 1)
            pool.affine_select(out=causal_bf[:, :], in_=causal_bf[:, :], compare_op=ALU.is_ge, fill=MASKED, base=0,
                               pattern=[[-1, P]], channel_multiplier=1).then_inc(consts_ok, 1)

            def deviation(ph, n, hf):
                pool.wait_ge(ph.var_ready, n + 1)
                pool.tensor_tensor(veps[:, hf, :], mv[:, hf, :, 1], eps_sb[:, :], ALU.add).then_inc(ph.eps_done, 1)
                pool.wait_ge(ph.eps_done, n + 1)
                pool.tensor_tensor(rstd[:, hf, :], veps[:, hf, :], minus_half[:, :], ALU.pow).then_inc(ph.rstd_ready, 1)

            def split(ph, prime, use, src, mid, low):
                pool.wait_ge(ph.rest_ready, prime + use + 1)
                pool.sem_inc(ph.rest_seen, 1)
                pool.tensor_copy(mid, src).then_inc(ph.mid_done, 1)
                pool.wait_ge(ph.mid_done, use + 1)
                pool.tensor_tensor(low, src, mid, ALU.subtract).then_inc(ph.parts_ready, 1)

            def dense_a(b, more):
                for hf in range(2):
                    for s in range(4):
                        split(A, 10, 10 * b + 4 * hf + s, rest[:, s], parts[:, s, 1, :], parts[:, s, 2, :])
                        if s == 1 and more:
                            deviation(A, 2 * (b + 1) + hf, hf)
                for c in range(2):
                    split(A, 10, 10 * b + 8 + c, restx[:, c], partsx[:, c, 1, :], partsx[:, c, 2, :])

            for hf in range(2):
                deviation(A, hf, hf)
            with pool.Fori(0, B - 1) as b:
                dense_a(b, True)
            dense_a(B - 1, False)

            def mask(q, b):
                v0, s = q // SA.NS, q % SA.NS
                if v0 >= 4 * B or s not in SA.diag:
                    return
                for p in range(2):
                    use = 2 * (SA.NS * v0 + s) + p
                    pool.wait_ge(SA.exp_done, 2 + use + 1 + 4 * b * 2 * SA.NS)
                    pool.sem_inc(SA.exp_seen, 1)
                    tri = probs[:, use % NPT, :, 0:P]
                    pool.affine_select(out=tri, in_=tri, compare_op=ALU.is_ge, fill=0.0, base=0,
                                       pattern=[[0, 2], [1, P]], channel_multiplier=-1).then_inc(SA.mask_done, 1)

            sequence(pool, SA, mask)

            def dense_c(b, more):
                for hf in range(2):
                    n = 2 * b + hf
                    if hf == 0 or more:
                        deviation(C, n + 1, 1 - hf)
                    for c in range(2):
                        split(C, 2, 2 * n + c, rest[:, c], parts[:, c, 1, :], parts[:, c, 2, :])

            deviation(C, 0, 0)
            with pool.Fori(0, B - 1) as b:
                dense_c(b, True)
            dense_c(B - 1, False)

            pool.wait_ge(w_late, 16 * 6)
            with pool.Fori(0, B) as b:
                for hf in range(2):
                    n = 2 * b + hf
                    deviation(E, n, hf)
                    pool.wait_ge(E.xn_done, 2 + 2 * n + 2)
                    pool.tensor_tensor(xt[:, hf], xn[:, hf], b2_sb[:, :].unsqueeze(1).to_broadcast([P, TT, D]),
                                       ALU.add).then_inc(xb_ready, 1)


_PRE = "L0_xattn_"
_INS = ["x", "ctx_1024"] + [_PRE + n for n in (
    "W_qkv", "W_self_out", "W_q", "W_kv", "W_cross_out", "W1", "b1", "W2", "b2",
    "ln1_scale", "ln1_bias", "ln2_scale", "ln2_bias", "ln3_scale", "ln3_bias")]


def kernel(**inputs):
    import numpy as _np
    import concourse.bacc as _bacc
    from concourse import mybir as _mybir
    from concourse.bass_utils import run_bass_kernel_spmd as _run

    nc = _bacc.Bacc("TRN2", target_bir_lowering=False, num_devices=1)
    arrays, args = {}, []
    for name in _INS:
        a = _np.ascontiguousarray(inputs[name])
        arrays[f"in_{name}_dram"] = a
        args.append(nc.dram_tensor(f"in_{name}_dram", a.shape, _mybir.dt.from_np(a.dtype), kind="ExternalInput").ap())
    shape = arrays["in_x_dram"].shape
    args.append(nc.dram_tensor("out_0_dram", shape, _mybir.dt.float32, kind="ExternalOutput").ap())
    decoder_block_kernel(nc, *args)
    r = _run(nc, [arrays], core_ids=[0])
    return r.results[0]["out_0_dram"]
```

```python
from contextlib import ExitStack

import concourse.bass as bass
from concourse import mybir

ALU = mybir.AluOpType
ACT = mybir.ActivationFunctionType
AX = mybir.AxisListType
F32 = mybir.dt.float32
BF16 = mybir.dt.bfloat16

P = 128
EPS = 1e-6
MASKED = -1e30
LOWEST = -3e38


def decoder_block_kernel(
    nc, x, ctx_in, w_qkv, w_self_out, w_q, w_kv, w_cross_out, w1, b1, w2, b2,
    ln1_s, ln1_b, ln2_s, ln2_b, ln3_s, ln3_b, out,
):
    B, L, D = x.shape
    LX = ctx_in.shape[1]
    F = w1.shape[1]
    H, DK = 16, 16
    SCALE = float(DK) ** -0.5
    KC = D // P
    FC = F // P
    HF = 512
    TT = HF // P
    NV = DK + 1
    KPX = LX // 2
    NPART = 3
    Q_PARTS, K_PARTS = (0, 0, 0, 1, 1, 2), (0, 1, 2, 0, 1, 0)
    NPROD = len(Q_PARTS)
    KROWS = NPROD * DK
    MROWS = P - NPART
    ONES_BF2 = 1.0019378662109375

    def dram(name, shape, dt):
        return nc.dram_tensor(name, shape, dt, kind="Internal").ap()

    q_parts = dram("q_parts", (2 * B, NPART, P, L), BF16)
    k_parts = dram("k_parts", (2 * B, NPART, P, L), BF16)
    v_aug = dram("v_aug", (B, L, H * NV), F32)
    qx_parts = dram("qx_parts", (2 * B, NPART, P, L), BF16)
    kx_parts = dram("kx_parts", (2 * B, NPART, P, LX), BF16)
    vx_aug = dram("vx_aug", (B, LX, H * NV), F32)
    self_ctx = dram("self_ctx", (2 * B, P, L), F32)
    cross_ctx = dram("cross_ctx", (2 * B, P, L), F32)
    x1_dram = dram("x1_dram", (B, L, D), F32)
    max_rows = dram("max_rows", (2, NPART, 32, P), BF16)

    def one(ap, i):
        return ap[bass.ds(i, 1)]

    def tokens(ap, b, hf):
        return one(ap, b).rearrange("b (h t p) d -> p (b h) t d", p=P, t=TT)[:, hf]

    with ExitStack() as ctx:
        def sb(name, shape, dt=F32):
            return ctx.enter_context(nc.sbuf_tensor(name, shape, dt))

        def sem(name):
            return ctx.enter_context(nc.semaphore(name))

        bank = ctx.enter_context(nc.psum_tensor("bank", [P, 8, HF], F32))

        wqkv_sb = sb("wqkv_sb", [P, KC, 3 * D])
        wso_sb = sb("wso_sb", [P, KC, D])
        wq_sb = sb("wq_sb", [P, KC, D])
        wkv_sb = sb("wkv_sb", [P, KC, 2 * D])
        wco_sb = sb("wco_sb", [P, KC, D])
        w1_sb = sb("w1_sb", [P, KC, F])
        w2_sb = sb("w2_sb", [P, FC, D])
        b1_sb = sb("b1_sb", [P, FC])
        b2_sb = sb("b2_sb", [P, D])
        lns_sb = sb("lns_sb", [P, 3, KC])
        lnb_sb = sb("lnb_sb", [P, 3, KC])
        ident = sb("ident", [P, P])
        ident_bf = sb("ident_bf", [P, P], BF16)
        causal_bf = sb("causal_bf", [P, P], BF16)
        minus_half = sb("minus_half", [P, TT])
        eps_sb = sb("eps_sb", [P, TT])
        zeros = sb("zeros", [32, P])
        rs = sb("rs", [P, 2, 16])

        xt = sb("xt", [P, 2, TT, D])
        out_mem = sb("out_mem", [P, 3 * 2 * HF])
        VCOLS = (L // P) * 8 * NV + 32 - NV
        nx_mem = sb("nx_mem", [P, 2 * VCOLS])
        vst_mem = sb("vst_mem", [P, 2 * TT * H * NV])
        xn = out_mem[:, 0:2 * TT * D].rearrange("p (h t d) -> p h t d", h=2, t=TT)
        nx = nx_mem[:, 0:2 * TT * D].rearrange("p (h t d) -> p h t d", h=2, t=TT)
        nxT = sb("nxT", [P, 2, KC, HF])
        cT = vst_mem[:, 0:2 * KC * HF].rearrange("p (h k t) -> p h k t", h=2, k=KC)
        stats = sb("stats", [P, 2, TT, 6])
        mv = sb("mv", [P, 2, TT, 2])
        veps = sb("veps", [P, 2, TT])
        rstd = sb("rstd", [P, 2, TT])
        parts = sb("parts", [P, 4, NPART, HF], BF16)
        vst = vst_mem[:, :].rearrange("p (a t h e) -> p a t h e", a=2, t=TT, h=H)
        cx = sb("cx", [KPX, 2, D])
        cxT = sb("cxT", [P, KC, LX])
        partsx = sb("partsx", [P, KC, NPART, LX], BF16)
        restx = sb("restx", [P, KC, LX])
        vstx = sb("vstx", [KPX, 2, H, NV])

        q_st = [sb(f"q_st{w}", [P, 4, L], BF16) for w in range(4)]
        k_st = [sb(f"k_st{w}", [P, 4, L], BF16) for w in range(4)]
        v_cur = [nx_mem[:, VCOLS * c:VCOLS * (c + 1)] for c in range(2)]
        NPT = 16
        probs = sb("probs", [P, NPT, HF])
        mx = sb("mx", [P, 2, 2, 32])
        mxc = sb("mxc", [P, 2, 32])
        nm = sb("nm", [32, 2, NPART, P], BF16)
        nmf = sb("nmf", [32, P])
        nmr = sb("nmr", [32, P])
        o_mem = [out_mem[:, 2 * HF * i:2 * HF * i + 2 * HF] for i in range(3)]
        oT = o_mem[0].rearrange("p (h c d) -> p h c d", h=2, d=32)
        oN = o_mem[1].rearrange("p (h c d) -> p h c d", h=2, d=32)
        oC = o_mem[2].rearrange("p (h t) -> p h t", h=2)
        rest = probs[:, FC:FC + 4, :]
        hT = probs[:, 0:FC, :]

        w_in = sem("w_in")
        w_late = sem("w_late")
        consts_ok = sem("consts_ok")
        pool_const = sem("pool_const")
        ones_ok, st_filled = sem("ones_ok"), sem("st_filled")

        class Dense:

            def __init__(self, n):
                self.x_in = [sem(f"{n}_x_in{i}") for i in range(2)]
                self.o_ready = sem(f"{n}_o_ready")
                self.xn_done = sem(f"{n}_xn_done")
                self.xn_stored = [sem(f"{n}_xn_stored{i}") for i in range(2)]
                self.stat_done, self.stat_seen = sem(f"{n}_stat_done"), sem(f"{n}_stat_seen")
                self.var_ready = sem(f"{n}_var_ready")
                self.eps_done = sem(f"{n}_eps_done")
                self.rstd_ready = sem(f"{n}_rstd_ready")
                self.nx_ready = sem(f"{n}_nx_ready")
                self.tp_ready = sem(f"{n}_tp_ready")
                self.nxT_ready = sem(f"{n}_nxT_ready")
                self.p_ready = sem(f"{n}_p_ready")
                self.hi_ready = sem(f"{n}_hi_ready")
                self.rest_ready = sem(f"{n}_rest_ready")
                self.mid_done = sem(f"{n}_mid_done")
                self.parts_ready = sem(f"{n}_parts_ready")
                self.parts_stored = [sem(f"{n}_parts_stored{i}") for i in range(4)]

        A, C, E = Dense("A"), Dense("C"), Dense("E")
        v_ready, v_evac = sem("v_ready"), sem("v_evac")
        v_stored = [sem(f"v_stored{i}") for i in range(2)]
        cx_in, ctp_ready, cxT_ready = sem("cx_in"), sem("ctp_ready"), sem("cxT_ready")
        px_stored = [sem(f"px_stored{i}") for i in range(2)]
        vx_stored = sem("vx_stored")
        h_ready, h_evac = sem("h_ready"), sem("h_evac")
        xb_ready = sem("xb_ready")
        f_ready, y_done = sem("f_ready"), sem("y_done")
        y_stored = [sem(f"y_stored{i}") for i in range(2)]

        class Attention:

            def __init__(self, n, causal, kp, nkb, qp, kp_dram, v_dram, out_dram, s_banks, acc, m_banks):
                self.causal, self.kp, self.nkb, self.nk = causal, kp, nkb, kp * nkb
                self.q_dram, self.k_dram, self.v_dram, self.out_dram = qp, kp_dram, v_dram, out_dram
                self.s_banks, self.acc, self.m_banks = s_banks, acc, m_banks
                self.SB, self.AB, self.MB = len(s_banks), len(acc), len(m_banks)
                self.steps = []
                for hf in range(2):
                    for kb in range(4 * (hf + 1) if causal else nkb):
                        lo = max(HF * hf, P * kb) if causal else HF * hf
                        self.steps.append((hf, kb, lo, HF * (hf + 1) - lo))
                self.NS = len(self.steps)
                self.tiles = []
                if causal:
                    for qb in range(8):
                        for k0 in range(0, P * (qb + 1), HF):
                            keys = min(P * (qb + 1) - k0, HF)
                            m = min(HF // keys, 4) if keys != 384 else 1
                            self.tiles += [(range(8 * i + qb, 8 * (i + m), 8), k0, keys, k0 // HF) for i in range(0, 4, m)]
                else:
                    m = HF // self.nk
                    self.tiles += [(range(j, min(j + m, 32)), 0, self.nk, 0) for j in range(0, 32, m)]
                self.MT = len(self.tiles)
                whole, upto = sum(x[3] for x in self.steps), 0
                self.beside = []
                for x in self.steps:
                    first, upto = upto * self.MT // whole, upto + x[3]
                    self.beside.append(range(first, upto * self.MT // whole))
                self.M0 = (len(self.beside[0]) + 1) // 2
                self.last = [max(s for s in range(self.NS) if self.steps[s][0] == hf) for hf in range(2)]
                self.diag = [s for s in range(self.NS) if causal and P * self.steps[s][1] >= HF * self.steps[s][0]]
                self.ND = 2 * len(self.diag)
                self.stack_in = [sem(f"{n}_stack_in{w}") for w in range(4)]
                self.v_in = [sem(f"{n}_v_in{c}") for c in range(2)]
                self.m_ready = sem(f"{n}_m_ready")
                self.m_free = sem(f"{n}_m_free")
                self.mxc_ready = sem(f"{n}_mxc_ready")
                self.nm_hi = sem(f"{n}_nm_hi")
                self.nmr_done = sem(f"{n}_nmr_done")
                self.nm_mid = sem(f"{n}_nm_mid")
                self.nm_ready = sem(f"{n}_nm_ready")
                self.rows_out = [sem(f"{n}_rows_out{i}") for i in range(2)]
                self.rows_in = [sem(f"{n}_rows_in{i}") for i in range(2)]
                self.st_ready = sem(f"{n}_st_ready")
                self.exp_done, self.exp_seen = sem(f"{n}_exp_done"), sem(f"{n}_exp_seen")
                self.mask_done = sem(f"{n}_mask_done")
                self.pv_done = sem(f"{n}_pv_done")
                self.acc_free = sem(f"{n}_acc_free")
                self.rs_done = sem(f"{n}_rs_done")
                self.oN_done = sem(f"{n}_oN_done")
                self.oC_ready = [sem(f"{n}_oC_ready{i}") for i in range(2)]
                self.oC_stored = [sem(f"{n}_oC_stored{i}") for i in range(2)]

            def tile_use(self, v, n):
                if isinstance(v, int) and v == 0:
                    return n
                return (self.MT + 1) * v + n - (n < self.M0)

            def turn_use(self, v):
                return (self.MT + 1) * (v + 1) - 1 + self.M0 * (v < 4 * B - 1)

        SA = Attention("S", True, P, L // P, q_parts, k_parts, v_aug, self_ctx, [0, 1, 2], [3], [4, 5, 6, 7])
        XA = Attention("X", False, KPX, 2, qx_parts, kx_parts, vx_aug, cross_ctx, [0, 1, 2, 3], [4], [5, 6, 7])

        LAG = 2
        TAIL = LAG + 1
        PROBS_STEPS = NPT // 4

        def fill_stacks(eng, w, filled):
            for st, value in ((q_st[w], 0.0), (k_st[w], ONES_BF2)):
                eng.memset(st[KROWS:P, :, :].rearrange("p i t -> p (i t)").bitcast(F32), value).then_inc(filled, 1)

        def sequence(eng, a, slot):
            per = 4 * a.NS
            for q in range(TAIL):
                slot(q, 0)
            with eng.Fori(0, B - 1) as b:
                for q in range(TAIL, TAIL + per):
                    slot(q, b)
            for q in range(TAIL + (B - 1) * per, B * per + TAIL):
                slot(q, 0)

        block = ctx.enter_context(nc.Block())

        @block.sync
        def _(sp):
            def load_x(ph, src, b, hf):
                sp.dma_start(xt[:, hf], tokens(src, b, hf)).then_inc(ph.x_in[hf], 16)

            def load_ctx(b):
                sp.dma_start(cx[:, :, :], one(ctx_in, b).rearrange("b (k p) d -> p (b k) d", p=KPX)).then_inc(cx_in, 16)

            for s in range(4):
                sp.sem_inc(A.parts_stored[s], 16)
            for s in range(2):
                sp.sem_inc(v_stored[s], 16)
                sp.sem_inc(px_stored[s], 16)
            sp.sem_inc(vx_stored, 16)
            for hf in range(2):
                load_x(A, x, 0, hf)
            load_ctx(0)

            def store_a(b, more):
                if more:
                    for hf in range(2):
                        sp.wait_ge(A.nx_ready, 2 * b + hf + 1)
                        load_x(A, x, b + 1, hf)
                for hf in range(2):
                    for s in range(4):
                        dst = (q_parts, k_parts)[s // 2]
                        sp.wait_ge(A.parts_ready, 10 * b + 4 * hf + s + 1)
                        sp.dma_start(one(dst, 2 * b + s % 2).rearrange("u s p t -> p (u s) t")[:, :, HF * hf:HF * hf + HF],
                                     parts[:, s]).then_inc(A.parts_stored[s], 16)
                    sp.wait_ge(v_evac, 2 + 5 * b + 2 * hf + 2)
                    sp.dma_start(tokens(v_aug, b, hf),
                                 vst[:, hf].rearrange("p t h e -> p t (h e)")).then_inc(v_stored[hf], 16)
                if more:
                    sp.wait_ge(ctp_ready, b + 1)
                    load_ctx(b + 1)
                for c in range(2):
                    sp.wait_ge(A.parts_ready, 10 * b + 8 + c + 1)
                    sp.dma_start(one(kx_parts, 2 * b + c).rearrange("u s p t -> p (u s) t"),
                                 partsx[:, c]).then_inc(px_stored[c], 16)
                sp.wait_ge(v_evac, 2 + 5 * b + 5)
                sp.dma_start(one(vx_aug, b).rearrange("b (k p) e -> p (b k) e", p=KPX),
                             vstx[:, :].rearrange("p k h e -> p k (h e)")).then_inc(vx_stored, 16)

            with sp.Fori(0, B - 1) as b:
                store_a(b, True)

            def load_stacks(a, v0, b, sides="qk"):
                w, u = v0 % 4, v0 // 2 + 2 * b
                for s in range(NPROD):
                    for side, st, src, part, n in (("q", q_st, a.q_dram, Q_PARTS[s], L), ("k", k_st, a.k_dram, K_PARTS[s], a.nk)):
                        if side in sides:
                            sp.dma_start(st[w][DK * s:DK * s + DK, :, 0:n],
                                         one(src, u).rearrange("u s (i g d) t -> d (u s) g i t", g=2, d=DK)[:, part, w % 2]
                                         ).then_inc(a.stack_in[w], 16)

            def load_values(a, v0, b):
                c = v0 % 4 // 2
                sp.dma_start(v_cur[c][0:a.kp, 0:a.nkb * 8 * NV].rearrange("p (k e) -> p k e", k=a.nkb),
                             one(a.v_dram, v0 // 4 + b).rearrange("b (k p) (c e) -> p (b k) c e", p=a.kp, c=2)[:, :, c]
                             ).then_inc(a.v_in[c], 16)

            for s in range(4):
                sp.wait_ge(A.parts_stored[s], 16 + 16 * 2)
            for v in range(3):
                load_stacks(SA, v, 0)
            store_a(B - 1, False)
            for s in range(4):
                sp.wait_ge(A.parts_stored[s], 16 + 16 * 2 * B)
            for s in range(2):
                sp.wait_ge(v_stored[s], 16 + 16 * B)
                sp.wait_ge(px_stored[s], 16 + 16 * B)
            sp.wait_ge(vx_stored, 16 + 16 * B)

            def attention(a, then):
                def rows(v0, b):
                    v, par = v0 + 4 * b, v0 % 2
                    sp.wait_ge(a.nm_ready, v + 1)
                    sp.dma_start(max_rows[par].rearrange("s r t -> r s t"), nm[:, par]).then_inc(a.rows_out[par], 16)
                    sp.wait_ge(a.rows_out[par], 16 * (v0 // 2 + 2 * b + 1))
                    sp.dma_start(q_st[v0 % 4][MROWS:P, :, :],
                                 max_rows[par].rearrange("s (i q) t -> s i (q t)", i=4)).then_inc(a.rows_in[par], 16)

                def store(v0, b):
                    u = v0 // 2 + 2 * b
                    for hf in range(2):
                        sp.wait_ge(a.oC_ready[hf], 1 + u + 1)
                        sp.dma_start(one(a.out_dram, u).rearrange("u p t -> p (u t)")[:, HF * hf:HF * hf + HF],
                                     oC[:, hf]).then_inc(a.oC_stored[hf], 16)

                def window(v0, b):
                    v = v0 + 4 * b
                    if v0 + 1 < 4 * B:
                        rows(v0 + 1, b)
                    if v0 + 3 < 4 * B:
                        sp.wait_ge(a.pv_done, PROBS_STEPS + a.NS * v)
                        load_stacks(a, v0 + 3, b)
                        if v0 % 2 == 0:
                            load_values(a, v0 + 3, b)
                    if v0 and v0 % 2 == 0:
                        store(v0 - 1, b)

                for hf in range(2):
                    sp.sem_inc(a.oC_stored[hf], 16)
                load_values(a, 1, 0)
                rows(0, 0)
                window(0, 0)
                with sp.Fori(0, B - 1) as b:
                    for w in range(1, 5):
                        window(w, b)
                for hf in range(2):
                    sp.wait_ge(a.oC_stored[hf], 16 + 16 * 2)
                then()
                for w in range(1, 4):
                    window(4 * (B - 1) + w, 0)
                store(4 * B - 1, 0)
                for hf in range(2):
                    sp.wait_ge(a.oC_stored[hf], 16 + 16 * 2 * B)

            def load_dense(ph, src, cdram, b, hf):
                load_x(ph, src, b, hf)
                sp.dma_start(cT[:, hf], cdram[bass.ds(2 * b, 2)].rearrange("c p t -> p c t")[:, :, HF * hf:HF * hf + HF]
                             ).then_inc(ph.x_in[hf], 16)

            def first_c():
                for hf in range(2):
                    load_dense(C, x, self_ctx, 0, hf)

            attention(SA, first_c)

            for s in range(2):
                sp.sem_inc(C.parts_stored[s], 16)
                sp.sem_inc(C.xn_stored[s], 16)
            for v in range(3):
                load_stacks(XA, v, 0, "k")

            def sums_c(b, hf, more):
                sp.wait_ge(C.xn_done, 2 + 2 * (2 * b + hf) + 2)
                sp.dma_start(tokens(x1_dram, b, hf), xn[:, hf]).then_inc(C.xn_stored[hf], 16)
                if more:
                    load_dense(C, x, self_ctx, b + 1, hf)

            def parts_c(b, hf):
                for c in range(2):
                    sp.wait_ge(C.parts_ready, 2 * (2 * b + hf) + c + 1)
                    sp.dma_start(one(qx_parts, 2 * b + c).rearrange("u s p t -> p (u s) t")[:, :, HF * hf:HF * hf + HF],
                                 parts[:, c]).then_inc(C.parts_stored[c], 16)

            for hf in range(2):
                sums_c(0, hf, True)
            with sp.Fori(0, B - 2) as b:
                for hf in range(2):
                    sums_c(b + 1, hf, True)
                    parts_c(b, hf)
            for hf in range(2):
                sums_c(B - 1, hf, False)
                parts_c(B - 2, hf)
            for s in range(2):
                sp.wait_ge(C.parts_stored[s], 16 + 16 * 2)
            for v in range(3):
                load_stacks(XA, v, 0, "q")
            for hf in range(2):
                parts_c(B - 1, hf)
            for s in range(2):
                sp.wait_ge(C.parts_stored[s], 16 + 16 * 2 * B)
                sp.wait_ge(C.xn_stored[s], 16 + 16 * B)

            def first_e():
                for hf in range(2):
                    load_dense(E, x1_dram, cross_ctx, 0, hf)

            for hf in range(2):
                sp.sem_inc(y_stored[hf], 16)
            attention(XA, first_e)

            def store_e(b, more):
                for hf in range(2):
                    n = 2 * b + hf
                    sp.wait_ge(y_done, 2 + 2 * n + 2)
                    sp.dma_start(tokens(out, b, hf), xn[:, hf]).then_inc(y_stored[hf], 16)
                    if more:
                        load_dense(E, x1_dram, cross_ctx, b + 1, hf)

            with sp.Fori(0, B - 1) as b:
                store_e(b, True)
            store_e(B - 1, False)
            for hf in range(2):
                sp.wait_ge(y_stored[hf], 16 + 16 * B)

        @block.tensor
        def _(pe):
            def transposes(ph, n, hf, b0):
                pe.wait_ge(ph.nx_ready, n + 1)
                for k in range(KC):
                    for t in range(TT):
                        last = pe.transpose(bank[:, b0 + k, P * t:P * t + P], nx[:, hf, t, P * k:P * k + P], ident[:, :])
                    last.then_inc(ph.tp_ready, 1)

            def project(dst, w, cols, src):
                for k in range(KC):
                    last = pe.matmul(dst, w[:, k, cols], src[:, k, :], start=(k == 0), stop=(k == KC - 1))
                return last

            pe.wait_ge(w_in, 16 * 9)
            pe.wait_ge(consts_ok, 3)

            def values_a(b, hf, i):
                pe.wait_ge(v_evac, 2 + 5 * b + ((0, -1), (1, 2))[hf][i])
                for t in range(2 * i, 2 * i + 2):
                    for k in range(KC):
                        last = pe.matmul(bank[:, 6 + i, D * (t % 2):D * (t % 2) + D], nxT[:, hf, k, P * t:P * t + P],
                                         wqkv_sb[:, k, 2 * D:3 * D], start=(k == 0), stop=(k == KC - 1))
                last.then_inc(v_ready, 1)

            def dense_a(b, more):
                for hf in range(2):
                    n = 2 * b + hf
                    pe.wait_ge(A.nxT_ready, 2 * n + 2)
                    for s in range(4):
                        before = 10 * b + s if hf else 10 * b - 10 + (8 if s < 2 else 4) + s
                        pe.wait_ge(A.rest_ready, 10 + before + 1)
                        project(bank[:, 2 + s], wqkv_sb, slice(P * s, P * s + P), nxT[:, hf]).then_inc(A.p_ready, 1)
                    if hf == 0:
                        pe.wait_ge(cx_in, 16 * b + 16)
                        for k in range(KC):
                            for kb in range(2):
                                last = pe.transpose(bank[:, 0, LX * k + KPX * kb:LX * k + KPX * kb + KPX],
                                                    cx[:, kb, P * k:P * k + P], ident[0:KPX, 0:KPX])
                        last.then_inc(ctp_ready, 1)
                    values_a(b, hf, 0)
                    if hf == 0:
                        pe.wait_ge(cxT_ready, b + 1)
                    if hf == 0 or more:
                        transposes(A, n + 1, 1 - hf, 0)
                    values_a(b, hf, 1)
                for c in range(2):
                    pe.wait_ge(A.rest_ready, 10 + 10 * b + 4 + c + 1)
                    project(bank[:, 2 + c, 0:LX], wkv_sb, slice(P * c, P * c + P), cxT).then_inc(A.p_ready, 1)
                pe.wait_ge(v_evac, 2 + 5 * b + 3)
                for kb in range(2):
                    for k in range(KC):
                        last = pe.matmul(bank[0:KPX, 6, D * kb:D * kb + D], cxT[:, k, KPX * kb:KPX * kb + KPX],
                                         wkv_sb[:, k, D:2 * D], start=(k == 0), stop=(k == KC - 1))
                last.then_inc(v_ready, 1)

            transposes(A, 0, 0, 0)
            with pe.Fori(0, B - 1) as b:
                dense_a(b, True)
            dense_a(B - 1, False)

            def attention(a):
                pe.sem_inc(a.pv_done, PROBS_STEPS)

                def max_tile(v0, b, n):
                    v, w = v0 + 4 * b, v0 % 4
                    blocks, k0, keys, _ = a.tiles[n]
                    use, m = a.tile_use(v, n), a.m_banks[a.tile_use(v0, n) % a.MB]
                    if n == 0:
                        pe.wait_ge(a.stack_in[w], 16 * 2 * NPROD * (v0 // 4 + b + 1))
                    if v0 or n >= a.MB:
                        pe.wait_ge(a.m_free, use - a.MB + 1)
                    for j, (i, qb) in enumerate(divmod(x, 8) for x in blocks):
                        masked = a.causal and k0 + keys == P * (qb + 1)
                        last = pe.matmul(bank[:, m, keys * j:keys * j + keys], q_st[w][0:MROWS, i, P * qb:P * qb + P],
                                         k_st[w][0:MROWS, i, k0:k0 + keys], start=True, stop=not masked)
                        if masked:
                            last = pe.matmul(bank[:, m, keys * j + keys - P:keys * j + keys], ident_bf[:, :], causal_bf[:, :],
                                             start=False, stop=True)
                    last.then_inc(a.m_ready, 1)

                def turn(v0, b):
                    v, par = v0 + 4 * b, v0 % 2
                    use, m = a.turn_use(v0) + 4 * b * (a.MT + 1), a.m_banks[a.turn_use(v0) % a.MB]
                    if a.causal:
                        pe.wait_ge(a.mxc_ready, v + 1)
                    pe.wait_ge(a.m_free, use - (min(a.M0, a.MB - 1) if v0 < 4 * B - 1 else 0))
                    src = mxc[:, par] if a.causal else mx[:, par, 0]
                    pe.transpose(bank[0:32, m, 0:P], src, ident[:, :]).then_inc(a.m_ready, 1)

                def scores(v0, b, s, i):
                    v, w = v0 + 4 * b, v0 % 4
                    hf, kb, lo, n = a.steps[s]
                    m = a.s_banks[(4 * (a.NS * v0 + s) + i) % a.SB]
                    if s == 0 and i == 0:
                        pe.wait_ge(a.rows_in[v0 % 2], 16 * (v0 // 2 + 2 * b + 1))
                    pe.wait_ge(a.exp_done, 4 * (a.NS * v + s) + i + 1)
                    pe.matmul(bank[0:a.kp, m, 0:n], k_st[w][:, i, a.kp * kb:a.kp * kb + a.kp],
                              q_st[w][:, i, lo:lo + n], start=True, stop=True).then_inc(a.st_ready, 1)

                def weigh(v0, b, s):
                    v, w = v0 + 4 * b, v0 % 4
                    hf, kb, lo, n = a.steps[s]
                    if s == 0 and w % 2 == 0:
                        pe.wait_ge(a.v_in[w // 2], 16 * (v0 // 4 + b + 1))
                    if kb == 0:
                        pe.wait_ge(a.acc_free, 2 + 2 * v + hf - a.AB + 1)
                    if s in a.diag:
                        pe.wait_ge(a.mask_done, a.ND * v + 2 * a.diag.index(s) + 2)
                    else:
                        pe.wait_ge(a.exp_done, a.SB + 4 * (a.NS * v + s) + 4)
                    for i in range(4):
                        pt = (4 * (a.NS * v0 + s) + i) % NPT
                        col = 8 * NV * kb + NV * (2 * i + w % 2)
                        last = pe.matmul(bank[32 * i:32 * i + 32, a.acc[hf % a.AB], lo - HF * hf:lo - HF * hf + n],
                                         v_cur[w // 2][0:a.kp, col:col + 32],
                                         probs[0:a.kp, pt, 0:n], start=(kb == 0), stop=(s == a.last[hf]))
                    last.then_inc(a.pv_done, 1)

                def slot(q, b):
                    v0, s = q // a.NS, q % a.NS
                    some = list(a.beside[s]) if v0 + 2 < 4 * B else []
                    for i in range(4):
                        if v0 < 4 * B:
                            scores(v0, b, s, i)
                        for n in some[(len(some) * i + 3) // 4:(len(some) * (i + 1) + 3) // 4]:
                            max_tile(v0 + 2, b, n)
                        if i == 1 and 0 <= q - LAG < 4 * B * a.NS:
                            weigh((q - LAG) // a.NS, b, (q - LAG) % a.NS)
                        if i == 1 and s == 0 and v0 + 1 < 4 * B:
                            turn(v0 + 1, b)

                for v in range(2):
                    for n in range(a.MT):
                        max_tile(v, 0, n)
                        if v and n == a.M0 - 1:
                            turn(0, 0)
                sequence(pe, a, slot)

            pe.wait_ge(v_evac, 2 + 5 * B)
            pe.wait_ge(A.rest_ready, 10 + 10 * B)
            pe.wait_ge(ones_ok, 6)
            pe.wait_ge(st_filled, 6)
            attention(SA)

            def out_project(ph, w, b, hf):
                n = 2 * b + hf
                pe.wait_ge(ph.x_in[hf], 32 * b + 32)
                for i in range(2):
                    pe.wait_ge(ph.xn_done, 2 + 2 * n + i - 1)
                    for t in range(2 * i, 2 * i + 2):
                        for k in range(KC):
                            last = pe.matmul(bank[:, i, D * (t % 2):D * (t % 2) + D], cT[:, hf, k, P * t:P * t + P], w[:, k, :],
                                             start=(k == 0), stop=(k == KC - 1))
                    last.then_inc(ph.o_ready, 1)

            def dense_c(b, more):
                for hf in range(2):
                    n = 2 * b + hf
                    transposes(C, n, hf, 2)
                    if more:
                        out_project(C, wso_sb, b + 1, hf)
                    pe.wait_ge(C.nxT_ready, 2 * n + 2)
                    for c in range(2):
                        pe.wait_ge(C.rest_ready, 2 + 2 * n + c - 1)
                        project(bank[:, 4 + c], wq_sb, slice(P * c, P * c + P), nxT[:, hf]).then_inc(C.p_ready, 1)

            pe.wait_ge(SA.acc_free, 2 + 2 * 4 * B)
            pe.wait_ge(SA.exp_done, SA.SB + 4 * 4 * B * SA.NS)
            pe.wait_ge(w_late, 16 * 6)
            out_project(C, wso_sb, 0, 0)
            out_project(C, wso_sb, 0, 1)
            with pe.Fori(0, B - 1) as b:
                dense_c(b, True)
            dense_c(B - 1, False)

            pe.wait_ge(C.rest_ready, 2 + 2 * 2 * B)
            attention(XA)

            def dense_e(b, more):
                for hf in range(2):
                    n = 2 * b + hf
                    pe.wait_ge(E.nxT_ready, 2 * n + 2)
                    for f in range(FC):
                        pe.wait_ge(h_evac, 2 + FC * n + f - 1)
                        project(bank[:, 4 + f % 2], w1_sb, slice(P * f, P * f + P), nxT[:, hf]).then_inc(h_ready, 1)
                    if hf == 0:
                        out_project(E, wco_sb, b, 1)
                    elif more:
                        out_project(E, wco_sb, b + 1, 0)
                    pe.wait_ge(h_evac, 2 + FC * n + FC)
                    for i in range(2):
                        pe.wait_ge(y_done, 2 + 2 * n + i - 1)
                        for t in range(2 * i, 2 * i + 2):
                            for f in range(FC):
                                last = pe.matmul(bank[:, 6 + i, D * (t % 2):D * (t % 2) + D], hT[:, f, P * t:P * t + P],
                                                 w2_sb[:, f, :], start=(f == 0), stop=(f == FC - 1))
                        last.then_inc(f_ready, 1)
                        if i == 0 and (hf == 0 or more):
                            transposes(E, n + 1, 1 - hf, 2)

            pe.wait_ge(XA.acc_free, 2 + 2 * 4 * B)
            pe.wait_ge(XA.exp_done, XA.SB + 4 * 4 * B * XA.NS)
            out_project(E, wco_sb, 0, 0)
            transposes(E, 0, 0, 2)
            with pe.Fori(0, B - 1) as b:
                dense_e(b, True)
            dense_e(B - 1, False)

        @block.scalar
        def _(act):
            act.dma_start(wqkv_sb[:, :, :], w_qkv.rearrange("(k p) n -> p k n", p=P)).then_inc(w_in, 16)
            act.dma_start(wkv_sb[:, :, :], w_kv.rearrange("(k p) n -> p k n", p=P)).then_inc(w_in, 16)
            with nc.allow_non_contiguous_dma(reason="vectors of 256 and 1024 elements"):
                for i, (s, z) in enumerate(((ln1_s, ln1_b), (ln2_s, ln2_b), (ln3_s, ln3_b))):
                    act.dma_start(lns_sb[:, i, :], s.rearrange("(k p) -> p k", p=P)).then_inc(w_in, 16)
                    act.dma_start(lnb_sb[:, i, :], z.rearrange("(k p) -> p k", p=P)).then_inc(w_in, 16)
                act.dma_start(b1_sb[:, :], b1.rearrange("(k p) -> p k", p=P)).then_inc(w_in, 16)
            act.dma_start(b2_sb[:, :], b2.partition_broadcast(P)).then_inc(w_late, 16)
            for dst, src in ((wso_sb, w_self_out), (wq_sb, w_q), (wco_sb, w_cross_out), (w1_sb, w1), (w2_sb, w2)):
                act.dma_start(dst[:, :, :], src.rearrange("(k p) n -> p k n", p=P)).then_inc(w_late, 16)

            act.sem_inc(v_evac, 2)
            act.sem_inc(h_evac, 2)
            act.sem_inc(SA.exp_done, SA.SB)
            act.sem_inc(XA.exp_done, XA.SB)

            def scaled(ph, i, n, hf, b0):
                for k in range(KC):
                    act.wait_ge(ph.tp_ready, 2 * n + k + 1)
                    act.activation(nxT[:, hf, k, :], bank[:, b0 + k, :], ACT.Identity, bias=lnb_sb[:, i, k:k + 1],
                                   scale=lns_sb[:, i, k:k + 1]).then_inc(ph.nxT_ready, 1)

            act.wait_ge(w_in, 16 * 9)
            act.wait_ge(ones_ok, 6)

            def high(ph, use, dst, src):
                act.wait_ge(ph.p_ready, use + 1)
                act.copy(dst, src).then_inc(ph.hi_ready, 1)

            def middle(ph, prime, use, dst, src):
                act.wait_ge(ph.rest_ready, prime + use + 1)
                act.copy(dst, src).then_inc(ph.mid_done, 1)

            def values_a(b, hf, i):
                act.wait_ge(v_ready, 5 * b + 2 * hf + i + 1)
                for t in range(2 * i, 2 * i + 2):
                    last = act.copy(vst[:, hf, t, :, 0:DK],
                                    bank[:, 6 + i, D * (t % 2):D * (t % 2) + D].rearrange("p (h d) -> p h d", d=DK))
                last.then_inc(v_evac, 1)

            def dense_a(b, more):
                for hf in range(2):
                    n = 2 * b + hf
                    for s in range(4):
                        act.wait_ge(A.parts_stored[s], 16 * n + 16)
                        high(A, 10 * b + 4 * hf + s, parts[:, s, 0, :], bank[:, 2 + s, :])
                        if s:
                            middle(A, 10, 10 * b + 4 * hf + s - 1, parts[:, s - 1, 1, :], rest[:, s - 1])
                    if hf == 0:
                        act.wait_ge(ctp_ready, b + 1)
                        act.copy(cxT[:, :, :], bank[:, 0, 0:KC * LX].rearrange("p (k t) -> p k t", k=KC)).then_inc(cxT_ready, 1)
                    middle(A, 10, 10 * b + 4 * hf + 3, parts[:, 3, 1, :], rest[:, 3])
                    act.wait_ge(v_stored[hf], 16 * b + 16)
                    values_a(b, hf, 0)
                    if hf == 0 or more:
                        scaled(A, 0, n + 1, 1 - hf, 0)
                    values_a(b, hf, 1)
                for c in range(2):
                    act.wait_ge(px_stored[c], 16 * b + 16)
                    high(A, 10 * b + 8 + c, partsx[:, c, 0, :], bank[:, 2 + c, 0:LX])
                for c in range(2):
                    middle(A, 10, 10 * b + 8 + c, partsx[:, c, 1, :], restx[:, c])
                act.wait_ge(vx_stored, 16 * b + 16)
                act.wait_ge(v_ready, 5 * b + 5)
                for kb in range(2):
                    last = act.copy(vstx[:, kb, :, 0:DK], bank[0:KPX, 6, D * kb:D * kb + D].rearrange("p (h d) -> p h d", d=DK))
                last.then_inc(v_evac, 1)

            scaled(A, 0, 0, 0, 0)
            with act.Fori(0, B - 1) as b:
                dense_a(b, True)
            dense_a(B - 1, False)

            def attention(a):
                def slot(q, b):
                    v0, s = q // a.NS, q % a.NS
                    if v0 >= 4 * B:
                        return
                    v = v0 + 4 * b
                    n = a.steps[s][3]
                    step = a.NS * v + s
                    act.wait_ge(a.pv_done, step + 1)
                    for i in range(4):
                        act.wait_ge(a.st_ready, 4 * step + i + 1)
                        use = 4 * (a.NS * v0 + s) + i
                        act.activation(probs[0:a.kp, use % NPT, 0:n], bank[0:a.kp, a.s_banks[use % a.SB], 0:n], ACT.Exp,
                                       scale=SCALE).then_inc(a.exp_done, 1)

                sequence(act, a, slot)

            attention(SA)

            with act.Fori(0, B) as b:
                for hf in range(2):
                    n = 2 * b + hf
                    scaled(C, 1, n, hf, 2)
                    for c in range(2):
                        act.wait_ge(C.parts_stored[c], 16 * n + 16)
                        high(C, 2 * n + c, parts[:, c, 0, :], bank[:, 4 + c, :])
                    for c in range(2):
                        middle(C, 2, 2 * n + c, parts[:, c, 1, :], rest[:, c])

            attention(XA)

            def dense_e(b, more):
                for hf in range(2):
                    n = 2 * b + hf
                    for f in range(FC):
                        act.wait_ge(h_ready, FC * n + f + 1)
                        act.activation(hT[:, f, :], bank[:, 4 + f % 2, :], ACT.Relu, bias=b1_sb[:, f:f + 1]).then_inc(h_evac, 1)
                    if hf == 0 or more:
                        scaled(E, 2, n + 1, 1 - hf, 2)

            scaled(E, 2, 0, 0, 2)
            with act.Fori(0, B - 1) as b:
                dense_e(b, True)
            dense_e(B - 1, False)

        @block.vector
        def _(dve):
            fill_stacks(dve, 0, ones_ok)
            dve.memset(vst[:, :, :, :, DK:NV].rearrange("p a t h e -> p (a t h) e"), 1.0).then_inc(ones_ok, 1)
            dve.memset(vstx[:, :, :, DK:NV].rearrange("p k h e -> p (k h) e"), 1.0).then_inc(ones_ok, 1)
            dve.memset(mx[:, :, :, :].rearrange("p a b c -> p (a b c)"), LOWEST).then_inc(ones_ok, 1)
            dve.memset(nx_mem[:, 2 * VCOLS - 32 + NV:2 * VCOLS], 0.0).then_inc(ones_ok, 1)

            for ph, k in ((A, 10), (C, 2)):
                dve.sem_inc(ph.rest_ready, k)
            for ph in (C, E):
                dve.sem_inc(ph.xn_done, 2)
            dve.sem_inc(y_done, 2)
            for a in (SA, XA):
                dve.sem_inc(a.acc_free, 2)
                for hf in range(2):
                    dve.sem_inc(a.oC_ready[hf], 1)

            def moments(ph, src, n, hf):
                for t in range(TT):
                    last = dve.bn_stats(stats[:, hf, t, :], src[:, hf, t, :])
                last.then_inc(ph.stat_done, 1)
                dve.wait_ge(ph.stat_done, n + 1)
                dve.sem_inc(ph.stat_seen, 1)
                for t in range(TT):
                    last = dve.bn_aggr(mv[:, hf, t, :], stats[:, hf, t, :])
                last.then_inc(ph.var_ready, 1)

            def normalize(ph, src, n, hf):
                dve.wait_ge(ph.rstd_ready, n + 1)
                for t in range(TT):
                    last = dve.tensor_scalar(nx[:, hf, t, :], src[:, hf, t, :], mv[:, hf, t, 0:1], rstd[:, hf, t:t + 1],
                                             ALU.subtract, ALU.mult)
                last.then_inc(ph.nx_ready, 1)

            def split(ph, use, dst, src, hi):
                dve.wait_ge(ph.hi_ready, use + 1)
                dve.tensor_tensor(dst, src, hi, ALU.subtract).then_inc(ph.rest_ready, 1)

            def norm_a(b, hf):
                dve.wait_ge(A.x_in[hf], 16 * b + 16)
                moments(A, xt, 2 * b + hf, hf)
                normalize(A, xt, 2 * b + hf, hf)

            def dense_a(b, more):
                for hf in range(2):
                    for s in range(4):
                        split(A, 10 * b + 4 * hf + s, rest[:, s], bank[:, 2 + s, :], parts[:, s, 0, :])
                    if more:
                        norm_a(b + 1, hf)
                for c in range(2):
                    split(A, 10 * b + 8 + c, restx[:, c], bank[:, 2 + c, 0:LX], partsx[:, c, 0, :])

            for hf in range(2):
                norm_a(0, hf)
            with dve.Fori(0, B - 1) as b:
                dense_a(b, True)
            dense_a(B - 1, False)

            def attention(a):
                def max_tile(v0, b, n):
                    v, par = v0 + 4 * b, v0 % 2
                    blocks, _, keys, part = a.tiles[n]
                    use, m = a.tile_use(v, n), a.m_banks[a.tile_use(v0, n) % a.MB]
                    dve.wait_ge(a.m_ready, use + 1)
                    dve.tensor_reduce(mx[:, par, part, blocks.start:blocks[-1] + 1:blocks.step],
                                      bank[:, m, 0:len(blocks) * keys].rearrange("p (q k) -> p q k", k=keys), AX.X, ALU.max
                                      ).then_inc(a.m_free, 1)
                    if a.causal and n == a.MT - 1:
                        dve.wait_ge(a.m_free, use + 1)
                        dve.tensor_tensor(mxc[:, par], mx[:, par, 0], mx[:, par, 1], ALU.max).then_inc(a.mxc_ready, 1)

                def negate(v0, b):
                    v = v0 + 4 * b
                    use, m = a.turn_use(v0) + 4 * b * (a.MT + 1), a.m_banks[a.turn_use(v0) % a.MB]
                    if v0:
                        dve.wait_ge(a.nm_ready, v)
                    dve.wait_ge(a.m_ready, use + 1)
                    dve.tensor_scalar(nmf[:, :], bank[0:32, m, 0:P], -1.0, None, ALU.mult).then_inc(a.m_free, 1)

                def turn_sums(v0, b, hf):
                    v = v0 + 4 * b
                    dve.wait_ge(a.oN_done, 2 + 2 * v + hf - 1)
                    dve.wait_ge(a.pv_done, PROBS_STEPS + a.NS * v + a.last[hf] + 1)
                    dve.transpose(oT[:, hf].rearrange("p c d -> p (c d)"), bank[:, a.acc[hf % a.AB], :]).then_inc(a.acc_free, 1)

                def invert(v0, b, hf):
                    n = 2 * (v0 + 4 * b) + hf
                    dve.wait_ge(a.acc_free, 2 + n + 1)
                    dve.reciprocal(rs[:, hf, :], oT[:, hf, :, DK]).then_inc(a.rs_done, 1)

                def turn_back(v0, b, hf):
                    v, u = v0 + 4 * b, v0 // 2 + 2 * b
                    dve.wait_ge(a.oN_done, 2 + 2 * v + hf + 1)
                    dve.wait_ge(a.oC_stored[hf], 16 * u + 16)
                    dve.transpose(oC[:, hf, :], oN[:, hf].rearrange("p c d -> p (c d)")).then_inc(a.oC_ready[hf], 1)

                def slot(q, b):
                    v0, s = q // a.NS, q % a.NS
                    some = a.beside[s] if v0 + 2 < 4 * B else []
                    cut = len(some) - len(some) // 2
                    for n in some[:cut]:
                        max_tile(v0 + 2, b, n)
                    if s == 0 and v0 + 1 < 4 * B:
                        negate(v0 + 1, b)
                    for hf in range(2):
                        v1, s1 = divmod(q - LAG, a.NS)
                        if 0 <= v1 < 4 * B and s1 == a.last[hf]:
                            turn_sums(v1, b, hf)
                        v1, s1 = divmod(q - TAIL, a.NS)
                        if v1 >= 0 and v1 % 2 and s1 == a.last[hf]:
                            turn_back(v1, b, hf)
                    for n in some[cut:]:
                        max_tile(v0 + 2, b, n)
                    for hf in range(2):
                        v1, s1 = divmod(q - LAG, a.NS)
                        if 0 <= v1 < 4 * B and s1 == a.last[hf]:
                            invert(v1, b, hf)

                for v in range(2):
                    for n in range(a.MT):
                        max_tile(v, 0, n)
                        if v and n == a.M0 - 1:
                            negate(0, 0)
                sequence(dve, a, slot)

            attention(SA)

            def residual(ph, b, hf):
                n = 2 * b + hf
                dve.wait_ge(ph.x_in[hf], 32 * b + 32)
                for i in range(2):
                    dve.wait_ge(ph.o_ready, 2 * n + i + 1)
                    dve.tensor_tensor(xn[:, hf, 2 * i:2 * i + 2, :], xt[:, hf, 2 * i:2 * i + 2, :],
                                      bank[:, i, :].rearrange("p (t d) -> p t d", t=2), ALU.add).then_inc(ph.xn_done, 1)
                dve.wait_ge(ph.xn_done, 2 + 2 * n + 2)
                moments(ph, xn, n, hf)

            def ahead_c(b, hf):
                dve.wait_ge(C.xn_stored[hf], 16 * b + 16)
                residual(C, b, hf)

            def dense_c(b, more):
                for hf in range(2):
                    n = 2 * b + hf
                    if hf == 0 or more:
                        normalize(C, xn, n + 1, 1 - hf)
                    if more:
                        ahead_c(b + 1, hf)
                    for c in range(2):
                        split(C, 2 * n + c, rest[:, c], bank[:, 4 + c, :], parts[:, c, 0, :])

            for hf in range(2):
                dve.wait_ge(SA.oC_stored[hf], 16 + 16 * 2 * B)
            for hf in range(2):
                ahead_c(0, hf)
            normalize(C, xn, 0, 0)
            with dve.Fori(0, B - 1) as b:
                dense_c(b, True)
            dense_c(B - 1, False)

            for hf in range(2):
                dve.wait_ge(C.xn_stored[hf], 16 + 16 * B)
            attention(XA)

            def ahead_e(b, hf):
                dve.wait_ge(y_stored[hf], 16 * b + 16)
                residual(E, b, hf)

            def dense_e(b, more):
                for hf in range(2):
                    n = 2 * b + hf
                    if hf == 0:
                        ahead_e(b, 1)
                        normalize(E, xn, n + 1, 1)
                    elif more:
                        ahead_e(b + 1, 0)
                        normalize(E, xn, n + 1, 0)
                    dve.wait_ge(xb_ready, n + 1)
                    for i in range(2):
                        dve.wait_ge(f_ready, 2 * n + i + 1)
                        dve.tensor_tensor(xn[:, hf, 2 * i:2 * i + 2, :], xt[:, hf, 2 * i:2 * i + 2, :],
                                          bank[:, 6 + i, :].rearrange("p (t d) -> p t d", t=2), ALU.add).then_inc(y_done, 1)

            for hf in range(2):
                dve.wait_ge(XA.oC_stored[hf], 16 + 16 * 2 * B)
            ahead_e(0, 0)
            normalize(E, xn, 0, 0)
            with dve.Fori(0, B - 1) as b:
                dense_e(b, True)
            dense_e(B - 1, False)

        @block.gpsimd
        def _(pool):
            fill_stacks(pool, 1, st_filled)
            pool.wait_ge(st_filled, 2)
            pool.memset(ident[:, :], 0.0).then_inc(pool_const, 1)
            pool.memset(ident_bf[:, :], 0.0).then_inc(pool_const, 1)
            pool.memset(causal_bf[:, :], 0.0).then_inc(pool_const, 1)
            pool.memset(minus_half[:, :], -0.5).then_inc(pool_const, 1)
            pool.memset(eps_sb[:, :], EPS).then_inc(pool_const, 1)
            pool.memset(zeros[:, :], 0.0).then_inc(pool_const, 1)
            pool.wait_ge(pool_const, 6)
            for t in (ident, ident_bf):
                pool.affine_select(out=t[:, :], in_=t[:, :], compare_op=ALU.not_equal, fill=1.0, base=0,
                                   pattern=[[1, P]], channel_multiplier=-1).then_inc(consts_ok, 1)
            pool.affine_select(out=causal_bf[:, :], in_=causal_bf[:, :], compare_op=ALU.is_ge, fill=MASKED, base=0,
                               pattern=[[-1, P]], channel_multiplier=1).then_inc(consts_ok, 1)

            def deviation(ph, n, hf):
                pool.wait_ge(ph.var_ready, n + 1)
                pool.tensor_tensor(veps[:, hf, :], mv[:, hf, :, 1], eps_sb[:, :], ALU.add).then_inc(ph.eps_done, 1)
                pool.wait_ge(ph.eps_done, n + 1)
                pool.tensor_tensor(rstd[:, hf, :], veps[:, hf, :], minus_half[:, :], ALU.pow).then_inc(ph.rstd_ready, 1)

            def lowest(ph, use, src, mid, low):
                pool.wait_ge(ph.mid_done, use + 1)
                pool.tensor_tensor(low, src, mid, ALU.subtract).then_inc(ph.parts_ready, 1)

            def dense_a(b, more):
                for hf in range(2):
                    for s in range(4):
                        lowest(A, 10 * b + 4 * hf + s, rest[:, s], parts[:, s, 1, :], parts[:, s, 2, :])
                        if s == 1 and more:
                            deviation(A, 2 * (b + 1) + hf, hf)
                for c in range(2):
                    lowest(A, 10 * b + 8 + c, restx[:, c], partsx[:, c, 1, :], partsx[:, c, 2, :])

            for hf in range(2):
                deviation(A, hf, hf)
            pool.wait_ge(A.rstd_ready, 2)
            for w in (2, 3):
                fill_stacks(pool, w, st_filled)
            pool.wait_ge(st_filled, 6)
            with pool.Fori(0, B - 1) as b:
                dense_a(b, True)
            dense_a(B - 1, False)

            for a in (SA, XA):
                pool.sem_inc(a.oN_done, 2)

            def attention(a):
                def mask(v0, b, s):
                    for p in range(2):
                        use = 4 * (a.NS * v0 + s) + 2 * p
                        pool.wait_ge(a.exp_done, a.SB + use + 2 + 4 * b * 4 * a.NS)
                        pool.sem_inc(a.exp_seen, 1)
                        tri = probs[:, use % NPT:use % NPT + 2, 0:P]
                        pool.affine_select(out=tri, in_=tri, compare_op=ALU.is_ge, fill=0.0, base=0,
                                           pattern=[[0, 2], [1, P]], channel_multiplier=-1).then_inc(a.mask_done, 1)

                def negated_parts(v0, b):
                    v, par = v0 + 4 * b, v0 % 2
                    if v0 >= 2:
                        pool.wait_ge(a.rows_in[par], 16 * (v0 // 2 + 2 * b))
                    pool.wait_ge(a.m_free, a.turn_use(v0) + 4 * b * (a.MT + 1) + 1)
                    pool.tensor_tensor(nm[:, par, 0, :], nmf[:, :], zeros[:, :], ALU.add).then_inc(a.nm_hi, 1)
                    pool.wait_ge(a.nm_hi, v + 1)
                    pool.tensor_tensor(nmr[:, :], nmf[:, :], nm[:, par, 0, :], ALU.subtract).then_inc(a.nmr_done, 1)
                    pool.wait_ge(a.nmr_done, v + 1)
                    pool.tensor_tensor(nm[:, par, 1, :], nmr[:, :], zeros[:, :], ALU.add).then_inc(a.nm_mid, 1)
                    pool.wait_ge(a.nm_mid, v + 1)
                    pool.tensor_tensor(nm[:, par, 2, :], nmr[:, :], nm[:, par, 1, :], ALU.subtract).then_inc(a.nm_ready, 1)

                def divide(v0, b, hf):
                    v, g, u = v0 + 4 * b, v0 % 2, v0 // 2 + 2 * b
                    if not g:
                        pool.wait_ge(a.oC_ready[hf], 1 + u)
                    pool.wait_ge(a.rs_done, 2 * v + hf + 1)
                    pool.tensor_tensor(oN[:, hf, :, DK * g:DK * g + DK], oT[:, hf, :, 0:DK],
                                       rs[:, hf, :].unsqueeze(2).to_broadcast([P, 16, DK]), ALU.mult).then_inc(a.oN_done, 1)

                def slot(q, b):
                    v0, s = q // a.NS, q % a.NS
                    for hf in range(2):
                        v1, s1 = divmod(q - LAG, a.NS)
                        if 0 <= v1 < 4 * B and s1 == a.last[hf]:
                            divide(v1, b, hf)
                    if v0 < 4 * B and s in a.diag:
                        mask(v0, b, s)
                    if s == 0 and v0 + 1 < 4 * B:
                        negated_parts(v0 + 1, b)

                negated_parts(0, 0)
                sequence(pool, a, slot)

            attention(SA)

            def dense_c(b, more):
                for hf in range(2):
                    n = 2 * b + hf
                    if more:
                        deviation(C, n + 2, hf)
                    for c in range(2):
                        lowest(C, 2 * n + c, rest[:, c], parts[:, c, 1, :], parts[:, c, 2, :])

            for hf in range(2):
                deviation(C, hf, hf)
            with pool.Fori(0, B - 1) as b:
                dense_c(b, True)
            dense_c(B - 1, False)

            attention(XA)

            pool.wait_ge(w_late, 16 * 6)
            with pool.Fori(0, B) as b:
                for hf in range(2):
                    n = 2 * b + hf
                    deviation(E, n, hf)
                    pool.wait_ge(E.xn_done, 2 + 2 * n + 2)
                    pool.tensor_tensor(xt[:, hf], xn[:, hf], b2_sb[:, :].unsqueeze(1).to_broadcast([P, TT, D]),
                                       ALU.add).then_inc(xb_ready, 1)


_PRE = "L0_xattn_"
_INS = ["x", "ctx_1024"] + [_PRE + n for n in (
    "W_qkv", "W_self_out", "W_q", "W_kv", "W_cross_out", "W1", "b1", "W2", "b2",
    "ln1_scale", "ln1_bias", "ln2_scale", "ln2_bias", "ln3_scale", "ln3_bias")]


def kernel(**inputs):
    import numpy as _np
    import concourse.bacc as _bacc
    from concourse import mybir as _mybir
    from concourse.bass_utils import run_bass_kernel_spmd as _run

    nc = _bacc.Bacc("TRN2", target_bir_lowering=False, num_devices=1)
    arrays, args = {}, []
    for name in _INS:
        a = _np.ascontiguousarray(inputs[name])
        arrays[f"in_{name}_dram"] = a
        args.append(nc.dram_tensor(f"in_{name}_dram", a.shape, _mybir.dt.from_np(a.dtype), kind="ExternalInput").ap())
    shape = arrays["in_x_dram"].shape
    args.append(nc.dram_tensor("out_0_dram", shape, _mybir.dt.float32, kind="ExternalOutput").ap())
    decoder_block_kernel(nc, *args)
    r = _run(nc, [arrays], core_ids=[0])
    return r.results[0]["out_0_dram"]
```

```python
from contextlib import ExitStack

import concourse.bass as bass
from concourse import mybir

ALU = mybir.AluOpType
ACT = mybir.ActivationFunctionType
AX = mybir.AxisListType
F32 = mybir.dt.float32
BF16 = mybir.dt.bfloat16
F32R = mybir.dt.float32r

P = 128
EPS = 1e-6
MASKED = -1e30
LOWEST = -3e38


def decoder_block_kernel(
    nc, x, ctx_in, w_qkv, w_self_out, w_q, w_kv, w_cross_out, w1, b1, w2, b2,
    ln1_s, ln1_b, ln2_s, ln2_b, ln3_s, ln3_b, out,
):
    B, L, D = x.shape
    LX = ctx_in.shape[1]
    F = w1.shape[1]
    H, DK = 16, 16
    SCALE = float(DK) ** -0.5
    KC = D // P
    FC = F // P
    HF = 512
    TT = HF // P
    NV = DK + 1
    KPX = LX // 2
    NPART = 3
    Q_PARTS, K_PARTS = (0, 0, 0, 1, 1, 2), (0, 1, 2, 0, 1, 0)
    NPROD = len(Q_PARTS)
    RUNS = {"q": [(Q_PARTS.index(p), p, Q_PARTS.count(p)) for p in range(NPART)],
            "k": [(Q_PARTS.index(p), 0, Q_PARTS.count(p)) for p in range(NPART)]}
    KROWS = NPROD * DK
    MROWS = P - NPART
    ONES_BF2 = 1.0019378662109375

    def dram(name, shape, dt):
        return nc.dram_tensor(name, shape, dt, kind="Internal").ap()

    q_parts = dram("q_parts", (2 * B, NPART, P, L), BF16)
    k_parts = dram("k_parts", (2 * B, NPART, P, L), BF16)
    v_aug = dram("v_aug", (B, L, H * NV), F32)
    qx_parts = dram("qx_parts", (2 * B, NPART, P, L), BF16)
    kx_parts = dram("kx_parts", (2 * B, NPART, P, LX), BF16)
    vx_aug = dram("vx_aug", (B, LX, H * NV), F32)
    self_ctx = dram("self_ctx", (2 * B, P, L), F32)
    cross_ctx = dram("cross_ctx", (2 * B, P, L), F32)
    x1_dram = dram("x1_dram", (B, L, D), F32)
    max_rows = dram("max_rows", (2, NPART, 32, P), BF16)

    def one(ap, i):
        return ap[bass.ds(i, 1)]

    def tokens(ap, b, hf):
        return one(ap, b).rearrange("b (h t p) d -> p (b h) t d", p=P, t=TT)[:, hf]

    with ExitStack() as ctx:
        def sb(name, shape, dt=F32):
            return ctx.enter_context(nc.sbuf_tensor(name, shape, dt))

        def sem(name):
            return ctx.enter_context(nc.semaphore(name))

        bank = ctx.enter_context(nc.psum_tensor("bank", [P, 8, HF], F32))

        wqkv_sb = sb("wqkv_sb", [P, KC, 3 * D])
        wso_sb = sb("wso_sb", [P, KC, D])
        wq_sb = sb("wq_sb", [P, KC, D])
        wkv_sb = sb("wkv_sb", [P, KC, 2 * D])
        wco_sb = sb("wco_sb", [P, KC, D])
        with ExitStack() as early:
            def sb_early(name, shape):
                return early.enter_context(nc.sbuf_tensor(name, shape, F32R))

            wqk_hi, wqk_lo = sb_early("wqk_hi", [P, KC, 2 * D]), sb_early("wqk_lo", [P, KC, 2 * D])
            wv_hi, wv_lo = sb_early("wv_hi", [P, KC, D]), sb_early("wv_lo", [P, KC, D])
            wkx_hi, wkx_lo = sb_early("wkx_hi", [P, KC, D]), sb_early("wkx_lo", [P, KC, D])
        w1_sb = sb("w1_sb", [P, KC, F])
        w2_sb = sb("w2_sb", [P, FC, D])
        b1_sb = sb("b1_sb", [P, FC])
        b2_sb = sb("b2_sb", [P, D])
        lns_sb = sb("lns_sb", [P, 3, KC])
        lnb_sb = sb("lnb_sb", [P, 3, KC])
        ident = sb("ident", [P, P])
        ident_bf = sb("ident_bf", [P, P], BF16)
        causal_bf = sb("causal_bf", [P, P], BF16)
        minus_half = sb("minus_half", [P, TT])
        eps_sb = sb("eps_sb", [P, TT])
        zeros = sb("zeros", [32, P])
        rs = sb("rs", [P, 2, 16])

        xt = sb("xt", [P, 2, TT, D])
        out_mem = sb("out_mem", [P, 3 * 2 * HF])
        VCOLS = (L // P) * 8 * NV + 32 - NV
        nx_mem = sb("nx_mem", [P, 2 * VCOLS])
        vst_mem = sb("vst_mem", [P, 2 * TT * H * NV])
        nx = nx_mem[:, 0:2 * TT * D].rearrange("p (h t d) -> p h t d", h=2, t=TT)
        nxT = sb("nxT", [P, 2, KC, HF])
        xn = sb("xn", [P, 2, TT, D])
        cT = vst_mem[:, 0:2 * KC * HF].rearrange("p (h k t) -> p h k t", h=2, k=KC)
        stats = sb("stats", [P, 2, TT, 6])
        mv = sb("mv", [P, 2, TT, 2])
        veps = sb("veps", [P, 2, TT])
        rstd = sb("rstd", [P, 2, TT])
        vst = vst_mem[:, :].rearrange("p (a t h e) -> p a t h e", a=2, t=TT, h=H)

        v_cur = [nx_mem[:, VCOLS * c:VCOLS * (c + 1)] for c in range(2)]
        mx = sb("mx", [P, 2, 2, 32])
        mxc = sb("mxc", [P, 2, 32])
        nm = sb("nm", [32, 2, NPART, P], BF16)
        nmf = sb("nmf", [32, P])
        nmr = sb("nmr", [32, P])
        o_mem = [out_mem[:, 2 * HF * i:2 * HF * i + 2 * HF] for i in range(3)]
        oT = o_mem[0].rearrange("p (h c d) -> p h c d", h=2, d=32)
        oN = o_mem[1].rearrange("p (h c d) -> p h c d", h=2, d=32)
        oC = o_mem[2].rearrange("p (h t) -> p h t", h=2)

        with ExitStack() as room:
            def sb_room(name, shape, dt=F32):
                return room.enter_context(nc.sbuf_tensor(name, shape, dt))

            NPT = 16
            probs = sb_room("probs", [P, NPT, HF])
            parts = probs[:, 0:6, :].rearrange("p a t -> p (a t)").bitcast(BF16).rearrange("p (s c t) -> p s c t", s=4, c=NPART)
            rest = probs[:, FC:FC + 4, :]
            stacks = [(sb_room(f"q_st{w}", [P, 4, L], BF16), sb_room(f"k_st{w}", [P, 4, L], BF16)) for w in range(4)]
            q_st, k_st = [q for q, _ in stacks], [k for _, k in stacks]
            wvx_hi, wvx_lo = sb_room("wvx_hi", [P, KC, D], F32R), sb_room("wvx_lo", [P, KC, D], F32R)
            wqx_sb = sb_room("wqx_sb", [P, KC, D])
            cx = sb_room("cx", [KPX, 2, D])
            cxT = sb_room("cxT", [P, KC, LX])
            cxT_hi, cxT_lo = sb_room("cxT_hi", [P, KC, LX], F32R), sb_room("cxT_lo", [P, KC, LX], F32R)
            partsx = sb_room("partsx", [P, KC, NPART, LX], BF16)
            restx = sb_room("restx", [P, KC, LX])
            vstx = sb_room("vstx", [KPX, 2, H, NV])
        hT_hi, hT_lo = sb("hT_hi", [P, FC, HF], F32R), sb("hT_lo", [P, FC, HF], F32R)
        cT_hi, cT_lo = sb("cT_hi", [P, 2, KC, HF], F32R), sb("cT_lo", [P, 2, KC, HF], F32R)
        nT_hi, nT_lo = sb("nT_hi", [P, 2, KC, HF], F32R), sb("nT_lo", [P, 2, KC, HF], F32R)
        w1_hi, w1_lo = sb("w1_hi", [P, KC, F], F32R), sb("w1_lo", [P, KC, F], F32R)
        nxT_hi, nxT_lo = sb("nxT_hi", [P, 2, KC, HF], F32R), sb("nxT_lo", [P, 2, KC, HF], F32R)
        w2_hi, w2_lo = (t[:, :, :, :].rearrange("p h k (f d) -> p (h k f) d", d=D) for t in (nxT_hi, nxT_lo))
        wco_hi, wco_lo = sb("wco_hi", [P, KC, D], F32R), sb("wco_lo", [P, KC, D], F32R)
        HRING = 4
        hT = sb("hT", [P, HRING, HF])

        w_in = sem("w_in")
        w_late = sem("w_late")
        w_high_a, w_low_a, w_ordered = sem("w_high_a"), sem("w_low_a"), sem("w_ordered")
        w_ffn, w_qkv_in = sem("w_ffn"), sem("w_qkv_in")
        nxT_high_a, nxT_low_a, cxT_high, cxT_low = sem("nxT_high_a"), sem("nxT_low_a"), sem("cxT_high"), sem("cxT_low")
        consts_ok = sem("consts_ok")
        pool_const = sem("pool_const")
        ones_ok, st_filled = sem("ones_ok"), sem("st_filled")

        class Dense:

            def __init__(self, n, sums, stored):
                self.x_in = [sem(f"{n}_x_in{i}") for i in range(2)]
                if sums:
                    self.o_ready = sem(f"{n}_o_ready")
                    self.xn_done = sem(f"{n}_xn_done")
                self.stat_done, self.stat_seen = sem(f"{n}_stat_done"), sem(f"{n}_stat_seen")
                self.var_ready = sem(f"{n}_var_ready")
                self.eps_done = sem(f"{n}_eps_done")
                self.rstd_ready = sem(f"{n}_rstd_ready")
                self.nx_ready = sem(f"{n}_nx_ready")
                self.tp_ready = sem(f"{n}_tp_ready")
                self.nxT_ready = sem(f"{n}_nxT_ready")
                if stored:
                    self.p_ready = sem(f"{n}_p_ready")
                    self.hi_ready = sem(f"{n}_hi_ready")
                    self.rest_ready = sem(f"{n}_rest_ready")
                    self.mid_done = sem(f"{n}_mid_done")
                    self.parts_ready = sem(f"{n}_parts_ready")
                    self.parts_stored = [sem(f"{n}_parts_stored{i}") for i in range(stored)]

        A, C, E = Dense("A", False, 4), Dense("C", True, 2), Dense("E", True, 0)
        x1_stored = [sem(f"x1_stored{i}") for i in range(2)]
        v_ready, v_evac = sem("v_ready"), sem("v_evac")
        v_stored = [sem(f"v_stored{i}") for i in range(2)]
        cx_in, ctp_ready, cxT_ready = sem("cx_in"), sem("ctp_ready"), sem("cxT_ready")
        px_stored = [sem(f"px_stored{i}") for i in range(2)]
        vx_stored = sem("vx_stored")
        h_ready, h_evac = sem("h_ready"), sem("h_evac")
        h_hi, h_lo = sem("h_hi"), sem("h_lo")
        c_in = [sem(f"c_in{i}") for i in range(2)]
        c_hi, c_lo, nxT_high, nxT_low = sem("c_hi"), sem("c_lo"), sem("nxT_high"), sem("nxT_low")
        w_high, w_low = sem("w_high"), sem("w_low")
        xb_ready = sem("xb_ready")
        f_ready, y_done = sem("f_ready"), sem("y_done")
        y_stored = [sem(f"y_stored{i}") for i in range(2)]

        class Attention:

            def __init__(self, n, causal, kp, nkb, qp, kp_dram, v_dram, out_dram, s_banks, acc, m_banks):
                self.causal, self.kp, self.nkb, self.nk = causal, kp, nkb, kp * nkb
                self.q_dram, self.k_dram, self.v_dram, self.out_dram = qp, kp_dram, v_dram, out_dram
                self.s_banks, self.acc, self.m_banks = s_banks, acc, m_banks
                self.SB, self.AB, self.MB = len(s_banks), len(acc), len(m_banks)
                self.steps = []
                for hf in range(2):
                    for kb in range(4 * (hf + 1) if causal else nkb):
                        lo = max(HF * hf, P * kb) if causal else HF * hf
                        self.steps.append((hf, kb, lo, HF * (hf + 1) - lo))
                self.NS = len(self.steps)
                self.tiles = []
                if causal:
                    for qb in range(8):
                        for k0 in range(0, P * (qb + 1), HF):
                            keys = min(P * (qb + 1) - k0, HF)
                            m = min(HF // keys, 4) if keys != 384 else 1
                            self.tiles += [(range(8 * i + qb, 8 * (i + m), 8), k0, keys, k0 // HF) for i in range(0, 4, m)]
                else:
                    m = HF // self.nk
                    self.tiles += [(range(j, min(j + m, 32)), 0, self.nk, 0) for j in range(0, 32, m)]
                self.MT = len(self.tiles)
                whole, upto = sum(x[3] for x in self.steps), 0
                self.beside = []
                for x in self.steps:
                    first, upto = upto * self.MT // whole, upto + x[3]
                    self.beside.append(range(first, upto * self.MT // whole))
                self.M0 = (len(self.beside[0]) + 1) // 2
                self.last = [max(s for s in range(self.NS) if self.steps[s][0] == hf) for hf in range(2)]
                self.diag = [s for s in range(self.NS) if causal and P * self.steps[s][1] >= HF * self.steps[s][0]]
                self.ND = 2 * len(self.diag)
                self.stack_in = [sem(f"{n}_stack_in{w}") for w in range(4)]
                self.v_in = [sem(f"{n}_v_in{c}") for c in range(2)]
                self.m_ready = sem(f"{n}_m_ready")
                self.m_free = sem(f"{n}_m_free")
                if causal:
                    self.mxc_ready = sem(f"{n}_mxc_ready")
                    self.exp_seen = sem(f"{n}_exp_seen")
                    self.mask_done = sem(f"{n}_mask_done")
                self.nm_hi = sem(f"{n}_nm_hi")
                self.nmr_done = sem(f"{n}_nmr_done")
                self.nm_mid = sem(f"{n}_nm_mid")
                self.nm_ready = sem(f"{n}_nm_ready")
                self.rows_out = [sem(f"{n}_rows_out{i}") for i in range(2)]
                self.rows_in = [sem(f"{n}_rows_in{i}") for i in range(2)]
                self.st_ready = sem(f"{n}_st_ready")
                self.exp_done = sem(f"{n}_exp_done")
                self.pv_done = sem(f"{n}_pv_done")
                self.acc_free = sem(f"{n}_acc_free")
                self.rs_done = sem(f"{n}_rs_done")
                self.oN_done = sem(f"{n}_oN_done")
                self.oC_ready = [sem(f"{n}_oC_ready{i}") for i in range(2)]
                self.oC_stored = [sem(f"{n}_oC_stored{i}") for i in range(2)]

            def tile_use(self, v, n):
                if isinstance(v, int) and v == 0:
                    return n
                return (self.MT + 1) * v + n - (n < self.M0)

            def turn_use(self, v):
                return (self.MT + 1) * (v + 1) - 1 + self.M0 * (v < 4 * B - 1)

        SA = Attention("S", True, P, L // P, q_parts, k_parts, v_aug, self_ctx, [0, 1, 2], [3], [4, 5, 6, 7])
        XA = Attention("X", False, KPX, 2, qx_parts, kx_parts, vx_aug, cross_ctx, [0, 1, 2, 3], [4], [5, 6, 7])

        EARLY_BANKS, EARLY_SLOTS, EARLY_FROM = 3, 12, 6
        n_slots = 4 * EARLY_SLOTS - EARLY_FROM
        early_slots = [[]] * EARLY_FROM + [
            [(x // SA.MT, x % SA.MT) for x in range(2 * SA.MT * i // n_slots, 2 * SA.MT * (i + 1) // n_slots)]
            for i in range(n_slots)]

        LAG = 2
        TAIL = LAG + 1
        PROBS_STEPS = NPT // 4

        def order_heads(copy, dst, src, c, done):
            for k in range(KC):
                (copy)(
                    dst[:, k, P * c:P * c + P].rearrange("p (g d i) -> p g d i", g=2, d=DK),
                    src[:, k, P * c:P * c + P].rearrange("p (i g d) -> p g d i", g=2, d=DK)).then_inc(done, 1)

        def keys_of(a, w):
            return k_st[w][:, :, :].rearrange("p i t -> p (i t)")[:, 0:4 * a.nk].rearrange("p (i t) -> p i t", i=4)

        def fill_stacks(eng, w, filled):
            for st, value in ((q_st[w], 0.0), (k_st[w], ONES_BF2)):
                eng.memset(st[KROWS:P, :, :].rearrange("p i t -> p (i t)").bitcast(F32), value).then_inc(filled, 1)

        def sequence(eng, a, slot):
            per = 4 * a.NS
            for q in range(TAIL):
                slot(q, 0)
            with eng.Fori(0, B - 1) as b:
                for q in range(TAIL, TAIL + per):
                    slot(q, b)
            for q in range(TAIL + (B - 1) * per, B * per + TAIL):
                slot(q, 0)

        block = ctx.enter_context(nc.Block())

        @block.sync
        def _(sp):
            def load_x(ph, src, b, hf):
                sp.dma_start(xt[:, hf], tokens(src, b, hf)).then_inc(ph.x_in[hf], 16)

            def load_ctx(b):
                sp.dma_start(cx[:, :, :], one(ctx_in, b).rearrange("b (k p) d -> p (b k) d", p=KPX)).then_inc(cx_in, 16)

            for s in range(4):
                sp.sem_inc(A.parts_stored[s], 16)
            for s in range(2):
                sp.sem_inc(v_stored[s], 16)
                sp.sem_inc(px_stored[s], 16)
            sp.sem_inc(vx_stored, 16)
            load_x(A, x, 0, 0)
            with nc.allow_non_contiguous_dma(reason="vectors of 256 and 1024 elements"):
                for i, (s, z) in enumerate(((ln1_s, ln1_b), (ln2_s, ln2_b), (ln3_s, ln3_b))):
                    sp.dma_start(lns_sb[:, i, :], s.rearrange("(k p) -> p k", p=P)).then_inc(w_in, 16)
                    sp.dma_start(lnb_sb[:, i, :], z.rearrange("(k p) -> p k", p=P)).then_inc(w_in, 16)
                sp.dma_start(b1_sb[:, :], b1.rearrange("(k p) -> p k", p=P)).then_inc(w_in, 16)
            load_x(A, x, 0, 1)
            sp.dma_start(wkv_sb[:, :, :], w_kv.rearrange("(k p) n -> p k n", p=P)).then_inc(w_in, 16)
            load_ctx(0)
            sp.dma_start(b2_sb[:, :], b2.partition_broadcast(P)).then_inc(w_late, 16)
            for dst, src in ((wso_sb, w_self_out), (wq_sb, w_q), (wco_sb, w_cross_out)):
                sp.dma_start(dst[:, :, :], src.rearrange("(k p) n -> p k n", p=P)).then_inc(w_late, 16)

            def store_a(b, more, ahead, then=None):
                for hf in range(2):
                    for s in range(4):
                        dst = (q_parts, k_parts)[s // 2]
                        sp.wait_ge(A.parts_ready, 10 * b + 4 * hf + s + 1)
                        sp.dma_start(one(dst, 2 * b + s % 2).rearrange("u s p t -> p (u s) t")[:, :, HF * hf:HF * hf + HF],
                                     parts[:, s]).then_inc(A.parts_stored[s], 16)
                    sp.wait_ge(v_evac, 2 + 5 * b + 2 * hf + 2)
                    sp.dma_start(tokens(v_aug, b, hf),
                                 vst[:, hf].rearrange("p t h e -> p t (h e)")).then_inc(v_stored[hf], 16)
                    if ahead:
                        sp.wait_ge(A.nx_ready, 2 * b + 2 + hf + 1)
                        load_x(A, x, b + 2, hf)
                    if then:
                        then(hf)
                if more:
                    sp.wait_ge(ctp_ready, b + 1)
                    load_ctx(b + 1)
                for c in range(2):
                    sp.wait_ge(A.parts_ready, 10 * b + 8 + c + 1)
                    sp.dma_start(one(kx_parts, 2 * b + c).rearrange("u s p t -> p (u s) t"),
                                 partsx[:, c]).then_inc(px_stored[c], 16)
                sp.wait_ge(v_evac, 2 + 5 * b + 5)
                sp.dma_start(one(vx_aug, b).rearrange("b (k p) e -> p (b k) e", p=KPX),
                             vstx[:, :].rearrange("p k h e -> p k (h e)")).then_inc(vx_stored, 16)

            for hf in range(2):
                sp.wait_ge(A.nx_ready, hf + 1)
                load_x(A, x, 1, hf)
            with sp.Fori(0, B - 2) as b:
                store_a(b, True, True)

            def load_stacks(a, v0, b, sides="qk"):
                w, u = v0 % 4, v0 // 2 + 2 * b
                for side, st, src, n in (("q", q_st, a.q_dram, L), ("k", k_st, a.k_dram, a.nk)):
                    for r, first, count in RUNS[side] if side in sides else ():
                        rows = one(src, u).rearrange("u s (g d i) t -> (u s) g d (i t)", g=2, d=DK)[:, w % 2]
                        rows = rows[first:first + count] if side == "k" else rows[first:first + 1].to_broadcast([count, DK, 4 * n])
                        sp.dma_start(st[w][DK * r:DK * (r + count), :, :].rearrange("p i t -> p (i t)")[:, 0:4 * n],
                                     rows).then_inc(a.stack_in[w], 16)

            def load_values(a, v0, b):
                c = v0 % 4 // 2
                sp.dma_start(v_cur[c][0:a.kp, 0:a.nkb * 8 * NV].rearrange("p (k e) -> p k e", k=a.nkb),
                             one(a.v_dram, v0 // 4 + b).rearrange("b (k p) (c e) -> p (b k) c e", p=a.kp, c=2)[:, :, c]
                             ).then_inc(a.v_in[c], 16)

            def rows(a, v0, b):
                v, par = v0 + 4 * b, v0 % 2
                sp.wait_ge(a.nm_ready, v + 1)
                sp.dma_start(max_rows[par].rearrange("s r t -> r s t"), nm[:, par]).then_inc(a.rows_out[par], 16)
                sp.wait_ge(a.rows_out[par], 16 * (v0 // 2 + 2 * b + 1))
                sp.dma_start(q_st[v0 % 4][MROWS:P, :, :],
                             max_rows[par].rearrange("s (i q) t -> s i (q t)", i=4)).then_inc(a.rows_in[par], 16)

            for s in range(4):
                sp.wait_ge(A.parts_stored[s], 16 + 16 * 2)
            def second_stacks(hf):
                if hf == 0:
                    load_stacks(SA, 1, 0)

            def third_stacks(hf):
                if hf == 0:
                    rows(SA, 0, 0)
                    load_stacks(SA, 2, 0)
                else:
                    load_values(SA, 1, 0)

            load_stacks(SA, 0, 0)
            store_a(B - 2, True, False, second_stacks)
            store_a(B - 1, False, False, third_stacks)
            for s in range(4):
                sp.wait_ge(A.parts_stored[s], 16 + 16 * 2 * B)
            for s in range(2):
                sp.wait_ge(v_stored[s], 16 + 16 * B)
                sp.wait_ge(px_stored[s], 16 + 16 * B)
            sp.wait_ge(vx_stored, 16 + 16 * B)

            def attention(a, then, ahead):
                def store(v0, b):
                    u = v0 // 2 + 2 * b
                    for hf in range(2):
                        sp.wait_ge(a.oC_ready[hf], 1 + u + 1)
                        sp.dma_start(one(a.out_dram, u).rearrange("u p t -> p (u t)")[:, HF * hf:HF * hf + HF],
                                     oC[:, hf]).then_inc(a.oC_stored[hf], 16)

                def window(v0, b):
                    v = v0 + 4 * b
                    if v0 + 3 < 4 * B:
                        if v0:
                            sp.wait_ge(a.st_ready, 4 * a.NS * v)
                        load_stacks(a, v0 + 3, b)
                    if v0 + 1 < 4 * B:
                        rows(a, v0 + 1, b)
                    if v0 + 3 < 4 * B and v0 % 2 == 0:
                        sp.wait_ge(a.pv_done, PROBS_STEPS + a.NS * v)
                        load_values(a, v0 + 3, b)
                    if v0 and v0 % 2 == 0:
                        store(v0 - 1, b)

                for hf in range(2):
                    sp.sem_inc(a.oC_stored[hf], 16)
                if a is XA:
                    load_values(a, 1, 0)
                    rows(a, 0, 0)
                window(0, 0)
                with sp.Fori(0, B - 1) as b:
                    for w in range(1, 5):
                        window(w, b)
                for hf in range(2):
                    sp.wait_ge(a.oC_stored[hf], 16 + 16 * 2)
                then()
                for w in range(1, 4):
                    window(4 * (B - 1) + w, 0)
                for hf in range(2):
                    sp.wait_ge(a.oC_stored[hf], 16 + 16 * 2 * 2)
                ahead()
                store(4 * B - 1, 0)
                for hf in range(2):
                    sp.wait_ge(a.oC_stored[hf], 16 + 16 * 2 * B)

            def load_dense(ph, src, cdram, b, hf):
                load_x(ph, src, b, hf)
                sp.dma_start(cT[:, hf], cdram[bass.ds(2 * b, 2)].rearrange("c p t -> p c t")[:, :, HF * hf:HF * hf + HF]
                             ).then_inc(ph.x_in[hf], 16)

            def first_c():
                for hf in range(2):
                    load_dense(C, x, self_ctx, 0, hf)

            for s in range(2):
                sp.sem_inc(C.parts_stored[s], 16)
                sp.sem_inc(x1_stored[s], 16)
            def sums_c(b, hf, more):
                sp.wait_ge(C.xn_done, 2 + 2 * (2 * b + hf) + 2)
                sp.dma_start(tokens(x1_dram, b, hf), xn[:, hf]).then_inc(x1_stored[hf], 16)
                if more:
                    load_dense(C, x, self_ctx, b + 1, hf)

            def ahead_c():
                for hf in range(2):
                    sums_c(0, hf, True)

            attention(SA, first_c, ahead_c)

            for v in range(3):
                load_stacks(XA, v, 0, "k")

            def parts_c(b, hf):
                for c in range(2):
                    sp.wait_ge(C.parts_ready, 2 * (2 * b + hf) + c + 1)
                    sp.dma_start(one(qx_parts, 2 * b + c).rearrange("u s p t -> p (u s) t")[:, :, HF * hf:HF * hf + HF],
                                 parts[:, c]).then_inc(C.parts_stored[c], 16)

            with sp.Fori(0, B - 2) as b:
                for hf in range(2):
                    sums_c(b + 1, hf, True)
                    parts_c(b, hf)
            for hf in range(2):
                sums_c(B - 1, hf, False)
                parts_c(B - 2, hf)
            for s in range(2):
                sp.wait_ge(C.parts_stored[s], 16 + 16 * 2)
            for v in range(3):
                load_stacks(XA, v, 0, "q")
            for hf in range(2):
                parts_c(B - 1, hf)
            for s in range(2):
                sp.wait_ge(C.parts_stored[s], 16 + 16 * 2 * B)
                sp.wait_ge(x1_stored[s], 16 + 16 * B)

            def load_c(b, hf):
                sp.dma_start(cT[:, hf], cross_ctx[bass.ds(2 * b, 2)].rearrange("c p t -> p c t")[:, :, HF * hf:HF * hf + HF]
                             ).then_inc(c_in[hf], 16)

            def first_e():
                for hf in range(2):
                    load_x(E, x1_dram, 0, hf)
                    load_c(0, hf)

            for hf in range(2):
                sp.sem_inc(y_stored[hf], 16)
            attention(XA, first_e, lambda: None)

            def store_e(b, left):
                for hf in range(2):
                    n = 2 * b + hf
                    if left > hf:
                        sp.wait_ge(E.xn_done, 2 + 2 * n + 4)
                        load_c(b + 1 + hf, 1 - hf)
                    sp.wait_ge(y_done, 2 + 2 * n + 2)
                    sp.dma_start(tokens(out, b, hf), xn[:, hf]).then_inc(y_stored[hf], 16)
                    if left:
                        load_x(E, x1_dram, b + 1, hf)

            sp.wait_ge(E.xn_done, 2 + 2)
            load_c(1, 0)
            with sp.Fori(0, B - 2) as b:
                store_e(b, 2)
            store_e(B - 2, 1)
            store_e(B - 1, 0)
            for hf in range(2):
                sp.wait_ge(y_stored[hf], 16 + 16 * B)

        @block.tensor
        def _(pe):
            def transposes(ph, n, hf, b0):
                pe.wait_ge(ph.nx_ready, n + 1)
                for k in range(KC):
                    for t in range(TT):
                        last = pe.transpose(bank[:, b0 + k, P * t:P * t + P], nx[:, hf, t, P * k:P * k + P], ident[:, :])
                    last.then_inc(ph.tp_ready, 1)

            def project(dst, w, cols, src):
                for k in range(KC):
                    last = pe.matmul(dst, w[:, k, cols], src[:, k, :], start=(k == 0), stop=(k == KC - 1))
                return last

            def product(dst, terms, between=None):
                for j, (a_hi, a_lo, b_hi, b_lo) in enumerate(terms):
                    if between and j:
                        between(j - 1)
                    pe.matmul(dst, a_hi, b_lo, start=(j == 0), stop=False)
                    pe.matmul(dst, a_lo, b_hi, start=False, stop=False)
                    last = pe.matmul(dst, a_hi, b_hi, start=False, stop=(j == len(terms) - 1))
                return last

            def max_tile(a, v0, b, n, ring):
                v, w = v0 + 4 * b, v0 % 4
                blocks, k0, keys, _ = a.tiles[n]
                use, m = a.tile_use(v, n), a.m_banks[a.tile_use(v0, n) % ring]
                if n == 0:
                    pe.wait_ge(a.stack_in[w], 16 * 2 * NPART * (v0 // 4 + b + 1))
                    if v0 == 3 and a is SA:
                        pe.wait_ge(st_filled, 6)
                if v0 or n >= ring:
                    pe.wait_ge(a.m_free, use - ring + 1)
                for j, (i, qb) in enumerate(divmod(x, 8) for x in blocks):
                    masked = a.causal and k0 + keys == P * (qb + 1)
                    last = pe.matmul(bank[:, m, keys * j:keys * j + keys], q_st[w][0:MROWS, i, P * qb:P * qb + P],
                                     keys_of(a, w)[0:MROWS, i, k0:k0 + keys], start=True, stop=not masked)
                    if masked:
                        last = pe.matmul(bank[:, m, keys * j + keys - P:keys * j + keys], ident_bf[:, :], causal_bf[:, :],
                                         start=False, stop=True)
                last.then_inc(a.m_ready, 1)

            def turn(a, v0, b, ring):
                v, par = v0 + 4 * b, v0 % 2
                use, m = a.turn_use(v0) + 4 * b * (a.MT + 1), a.m_banks[a.turn_use(v0) % ring]
                if a.causal:
                    pe.wait_ge(a.mxc_ready, v + 1)
                pe.wait_ge(a.m_free, use - (min(a.M0, ring - 1) if v0 < 4 * B - 1 else 0))
                src = mxc[:, par] if a.causal else mx[:, par, 0]
                pe.transpose(bank[0:32, m, 0:P], src, ident[:, :]).then_inc(a.m_ready, 1)

            def first_tiles(a, tiles, ring):
                for v, n in tiles:
                    max_tile(a, v, 0, n, ring)
                    if v == 1 and n == a.M0 - 1:
                        turn(a, 0, 0, ring)

            pe.wait_ge(w_in, 16 * 8)
            pe.wait_ge(consts_ok, 3)

            def values_a(b, hf, i, between):
                pe.wait_ge(v_evac, 2 + 5 * b + 2 * hf + i)
                for t in range(2 * i, 2 * i + 2):
                    last = product(bank[:, 7, D * (t % 2):D * (t % 2) + D],
                                   [(nxT_hi[:, hf, k, P * t:P * t + P], nxT_lo[:, hf, k, P * t:P * t + P], wv_hi[:, k, :],
                                     wv_lo[:, k, :]) for k in range(KC)])
                    if t == 2 * i:
                        between(hf, 6 + 4 * i)
                last.then_inc(v_ready, 1)
                between(hf, 7 + 4 * i)

            def dense_a(b, more, early=None):
                def between(hf, j):
                    if early:
                        first_tiles(SA, early[EARLY_SLOTS * hf + j], EARLY_BANKS)

                for hf in range(2):
                    n = 2 * b + hf
                    if hf:
                        pe.wait_ge(cxT_ready, b + 1)
                    if hf == 0 or more:
                        pe.wait_ge(A.nxT_ready, KC * n + KC)
                        transposes(A, n + 1, 1 - hf, 0)
                    pe.wait_ge(w_low_a, 2 * D // P * KC)
                    pe.wait_ge(nxT_low_a, KC * n + KC)
                    for s in range(4):
                        use, j = 10 * b + 4 * hf + s, 2 * s if s < 3 else 8
                        pe.wait_ge(A.rest_ready, 10 + use - 1)
                        product(bank[:, 2 + s % 2], [(wqk_hi[:, k, P * s:P * s + P], wqk_lo[:, k, P * s:P * s + P],
                                                      nxT_hi[:, hf, k, :], nxT_lo[:, hf, k, :]) for k in range(KC)],
                                lambda _, j=j: between(hf, j)).then_inc(A.p_ready, 1)
                        between(hf, j + 1)
                        if s == 2:
                            pe.wait_ge(w_low_a, (2 * D // P + 1) * KC)
                            values_a(b, hf, 0, between)
                    if hf == 0:
                        pe.wait_ge(A.nxT_ready, KC * n + 2 * KC)
                        pe.wait_ge(cx_in, 16 * b + 16)
                        for k in range(KC):
                            for kb in range(2):
                                last = pe.transpose(bank[:, 0, LX * k + KPX * kb:LX * k + KPX * kb + KPX],
                                                    cx[:, kb, P * k:P * k + P], ident[0:KPX, 0:KPX])
                        last.then_inc(ctp_ready, 1)
                    values_a(b, hf, 1, between)
                pe.wait_ge(w_low_a, (3 * D // P + 2) * KC)
                pe.wait_ge(cxT_low, b + 1)
                for c in range(2):
                    pe.wait_ge(A.rest_ready, 10 + 10 * b + 8 + c - 1)
                    product(bank[:, 2 + c, 0:LX], [(wkx_hi[:, k, P * c:P * c + P], wkx_lo[:, k, P * c:P * c + P],
                                                    cxT_hi[:, k, :], cxT_lo[:, k, :]) for k in range(KC)]).then_inc(A.p_ready, 1)
                pe.wait_ge(v_evac, 2 + 5 * b + 4)
                for kb in range(2):
                    ks = slice(KPX * kb, KPX * kb + KPX)
                    last = product(bank[0:KPX, 7, D * kb:D * kb + D],
                                   [(cxT_hi[:, k, ks], cxT_lo[:, k, ks], wvx_hi[:, k, :], wvx_lo[:, k, :]) for k in range(KC)])
                last.then_inc(v_ready, 1)

            transposes(A, 0, 0, 0)
            with pe.Fori(0, B - 2) as b:
                dense_a(b, True)
            pe.wait_ge(ones_ok, 6)
            pe.wait_ge(st_filled, 4)
            dense_a(B - 2, True, early_slots[:2 * EARLY_SLOTS])
            dense_a(B - 1, False, early_slots[2 * EARLY_SLOTS:])

            def attention(a, ahead):
                pe.sem_inc(a.pv_done, PROBS_STEPS)

                def scores(v0, b, s, i):
                    v, w = v0 + 4 * b, v0 % 4
                    hf, kb, lo, n = a.steps[s]
                    m = a.s_banks[(4 * (a.NS * v0 + s) + i) % a.SB]
                    if s == 0 and i == 0:
                        pe.wait_ge(a.rows_in[v0 % 2], 16 * (v0 // 2 + 2 * b + 1))
                    pe.wait_ge(a.exp_done, 4 * (a.NS * v + s) + i + 1)
                    pe.matmul(bank[0:a.kp, m, 0:n], keys_of(a, w)[:, i, a.kp * kb:a.kp * kb + a.kp],
                              q_st[w][:, i, lo:lo + n], start=True, stop=True).then_inc(a.st_ready, 1)

                def weigh(v0, b, s):
                    v, w = v0 + 4 * b, v0 % 4
                    hf, kb, lo, n = a.steps[s]
                    if s == 0 and w % 2 == 0:
                        pe.wait_ge(a.v_in[w // 2], 16 * (v0 // 4 + b + 1))
                    if kb == 0:
                        pe.wait_ge(a.acc_free, 2 + 2 * v + hf - a.AB + 1)
                    if s in a.diag:
                        pe.wait_ge(a.mask_done, a.ND * v + 2 * a.diag.index(s) + 2)
                    else:
                        pe.wait_ge(a.exp_done, a.SB + 4 * (a.NS * v + s) + 4)
                    for i in range(4):
                        pt = (4 * (a.NS * v0 + s) + i) % NPT
                        col = 8 * NV * kb + NV * (2 * i + w % 2)
                        last = pe.matmul(bank[32 * i:32 * i + 32, a.acc[hf % a.AB], lo - HF * hf:lo - HF * hf + n],
                                         v_cur[w // 2][0:a.kp, col:col + 32],
                                         probs[0:a.kp, pt, 0:n], start=(kb == 0), stop=(s == a.last[hf]))
                    last.then_inc(a.pv_done, 1)

                def slot(q, b):
                    v0, s = q // a.NS, q % a.NS
                    some = list(a.beside[s]) if v0 + 2 < 4 * B else []
                    for i in range(4):
                        if v0 < 4 * B:
                            scores(v0, b, s, i)
                        for n in some[(len(some) * i + 3) // 4:(len(some) * (i + 1) + 3) // 4]:
                            max_tile(a, v0 + 2, b, n, a.MB)
                        if i == 1 and 0 <= q - LAG < 4 * B * a.NS:
                            weigh((q - LAG) // a.NS, b, (q - LAG) % a.NS)
                        if i == 1 and s == 0 and v0 + 1 < 4 * B:
                            turn(a, v0 + 1, b, a.MB)
                    if v0 >= 4 * B - 2:
                        ahead(q - (4 * B - 2) * a.NS)

                if a is XA:
                    first_tiles(a, [(v, n) for v in range(2) for n in range(a.MT)], a.MB)
                pe.wait_ge(a.m_free, 2 * a.MT + 1)
                sequence(pe, a, slot)

            pe.wait_ge(v_evac, 2 + 5 * B)
            pe.wait_ge(A.rest_ready, 10 + 10 * B)

            def project_c(b, hf, i):
                n = 2 * b + hf
                pe.wait_ge(C.x_in[hf], 32 * b + 32)
                pe.wait_ge(C.xn_done, 2 + 2 * n + i - 1)
                for t in range(2 * i, 2 * i + 2):
                    for k in range(KC):
                        last = pe.matmul(bank[:, 4 + i, D * (t % 2):D * (t % 2) + D], cT[:, hf, k, P * t:P * t + P],
                                         wso_sb[:, k, :], start=(k == 0), stop=(k == KC - 1))
                last.then_inc(C.o_ready, 1)

            def ahead_c(step):
                if step == 3:
                    pe.wait_ge(SA.m_free, (SA.MT + 1) * 4 * B)
                    pe.wait_ge(w_late, 16 * 4)
                if step in (3, 7, 11, 15):
                    project_c(0, step // 8, step // 4 % 2)

            attention(SA, ahead_c)

            def dense_c(b, more):
                for hf in range(2):
                    n = 2 * b + hf
                    transposes(C, n, hf, 6)
                    if more:
                        for i in range(2):
                            project_c(b + 1, hf, i)
                    pe.wait_ge(C.nxT_ready, 2 * n + 2)
                    for c in range(2):
                        pe.wait_ge(C.rest_ready, 2 + 2 * n + c - 1)
                        project(bank[:, c], wqx_sb, slice(P * c, P * c + P), nxT[:, hf]).then_inc(C.p_ready, 1)

            pe.wait_ge(SA.exp_done, SA.SB + 4 * 4 * B * SA.NS)
            pe.wait_ge(w_ordered, 2 * KC)
            with pe.Fori(0, B - 1) as b:
                dense_c(b, True)
            dense_c(B - 1, False)

            pe.wait_ge(C.rest_ready, 2 + 2 * 2 * B)
            pe.wait_ge(SA.acc_free, 2 + 2 * 4 * B)

            def project_e(b, hf, i, o_bank=4):
                n = 2 * b + hf
                pe.wait_ge(c_lo, n + 1)
                pe.wait_ge(E.xn_done, 2 + 2 * n + i - 1)
                for t in range(2 * i, 2 * i + 2):
                    last = product(bank[:, o_bank + i, D * (t % 2):D * (t % 2) + D],
                                   [(cT_hi[:, hf, k, P * t:P * t + P], cT_lo[:, hf, k, P * t:P * t + P], wco_hi[:, k, :],
                                     wco_lo[:, k, :]) for k in range(KC)])
                last.then_inc(E.o_ready, 1)

            def ahead_e(step):
                if step == 2:
                    pe.wait_ge(XA.m_free, (XA.MT + 1) * 4 * B)
                    pe.wait_ge(w_low, 1)
                if step in (2, 3):
                    project_e(0, 0, step - 2, 6)
                if step == 7:
                    transposes(E, 0, 0, 6)

            attention(XA, ahead_e)

            def dense_e(b, more):
                for hf in range(2):
                    n = 2 * b + hf
                    pe.wait_ge(nxT_low, 2 * n + 2)
                    for f in range(FC):
                        pe.wait_ge(h_evac, 2 + FC * n + f - 1)
                        product(bank[:, f % 2], [(w1_hi[:, k, P * f:P * f + P], w1_lo[:, k, P * f:P * f + P],
                                                  nT_hi[:, hf, k, :], nT_lo[:, hf, k, :]) for k in range(KC)]
                                ).then_inc(h_ready, 1)
                    if hf == 0 or more:
                        pe.wait_ge(XA.acc_free, 2 + 2 * 4 * B)
                        for i in range(2):
                            project_e(b + hf, 1 - hf, i)
                    pe.wait_ge(w_low, 3)
                    pe.wait_ge(h_lo, HRING + FC * n + FC)
                    for i in range(2):
                        pe.wait_ge(y_done, 2 + 2 * n + i - 1)
                        for t in range(2 * i, 2 * i + 2):
                            last = product(bank[:, 6 + i, D * (t % 2):D * (t % 2) + D],
                                           [(hT_hi[:, f, P * t:P * t + P], hT_lo[:, f, P * t:P * t + P], w2_hi[:, f, :], w2_lo[:, f, :])
                                            for f in range(FC)])
                        last.then_inc(f_ready, 1)
                        if i == 0 and (hf == 0 or more):
                            transposes(E, n + 1, 1 - hf, 2)

            pe.wait_ge(XA.exp_done, XA.SB + 4 * 4 * B * XA.NS)
            pe.wait_ge(w_low, 2)
            with pe.Fori(0, B - 1) as b:
                dense_e(b, True)
            dense_e(B - 1, False)

        @block.scalar
        def _(act):
            act.dma_start(wqkv_sb[:, :, :], w_qkv.rearrange("(k p) n -> p k n", p=P)).then_inc(w_qkv_in, 16)
            act.sem_inc(v_evac, 2)
            act.sem_inc(h_evac, 2)
            act.sem_inc(SA.exp_done, SA.SB)
            act.sem_inc(XA.exp_done, XA.SB)

            def scaled(ph, i, n, hf, b0):
                for k in range(KC):
                    act.wait_ge(ph.tp_ready, 2 * n + k + 1)
                    act.activation(nxT[:, hf, k, :], bank[:, b0 + k, :], ACT.Identity, bias=lnb_sb[:, i, k:k + 1],
                                   scale=lns_sb[:, i, k:k + 1]).then_inc(ph.nxT_ready, 1)


            def high(ph, use, dst, src):
                act.wait_ge(ph.p_ready, use + 1)
                act.copy(dst, src).then_inc(ph.hi_ready, 1)

            def middle(ph, prime, use, dst, src):
                act.wait_ge(ph.rest_ready, prime + use + 1)
                act.copy(dst, src).then_inc(ph.mid_done, 1)

            def values_a(b, hf, i):
                act.wait_ge(v_ready, 5 * b + 2 * hf + i + 1)
                for t in range(2 * i, 2 * i + 2):
                    last = act.copy(vst[:, hf, t, :, 0:DK],
                                    bank[:, 7, D * (t % 2):D * (t % 2) + D].rearrange("p (h d) -> p h d", d=DK))
                last.then_inc(v_evac, 1)

            def tokens_high(n, hf, k):
                act.wait_ge(A.nxT_ready, KC * n + k + 1)
                act.copy(nxT_hi[:, hf, k, :], nxT[:, hf, k, :]).then_inc(nxT_high_a, 1)

            def dense_a(b, more):
                for hf in range(2):
                    n = 2 * b + hf
                    ahead = hf == 0 or more
                    for s in range(4):
                        act.wait_ge(A.parts_stored[s], 16 * n + 16)
                        high(A, 10 * b + 4 * hf + s, parts[:, s, 0, :], bank[:, 2 + s % 2, :])
                        if s == 0 and ahead:
                            scaled(A, 0, n + 1, 1 - hf, 0)
                        if s:
                            middle(A, 10, 10 * b + 4 * hf + s - 1, parts[:, s - 1, 1, :], rest[:, s - 1])
                        if s in (1, 2) and ahead:
                            tokens_high(n + 1, 1 - hf, s - 1)
                        if s == 2:
                            act.wait_ge(v_stored[hf], 16 * b + 16)
                            values_a(b, hf, 0)
                    if hf == 0:
                        act.wait_ge(ctp_ready, b + 1)
                        act.copy(cxT[:, :, :], bank[:, 0, 0:KC * LX].rearrange("p (k t) -> p k t", k=KC)).then_inc(cxT_ready, 1)
                    middle(A, 10, 10 * b + 4 * hf + 3, parts[:, 3, 1, :], rest[:, 3])
                    if hf == 0:
                        act.wait_ge(cxT_ready, b + 1)
                        act.copy(cxT_hi[:, :, :], cxT[:, :, :]).then_inc(cxT_high, 1)
                    values_a(b, hf, 1)
                for c in range(2):
                    act.wait_ge(px_stored[c], 16 * b + 16)
                    high(A, 10 * b + 8 + c, partsx[:, c, 0, :], bank[:, 2 + c, 0:LX])
                for c in range(2):
                    middle(A, 10, 10 * b + 8 + c, partsx[:, c, 1, :], restx[:, c])
                act.wait_ge(vx_stored, 16 * b + 16)
                act.wait_ge(v_ready, 5 * b + 5)
                for kb in range(2):
                    last = act.copy(vstx[:, kb, :, 0:DK], bank[0:KPX, 7, D * kb:D * kb + D].rearrange("p (h d) -> p h d", d=DK))
                last.then_inc(v_evac, 1)

            act.wait_ge(w_qkv_in, 16)
            for c in range(4):
                order_heads(act.copy, wqk_hi, wqkv_sb, c, w_high_a)
            for k in range(KC):
                act.copy(wv_hi[:, k, :], wqkv_sb[:, k, 2 * D:3 * D]).then_inc(w_high_a, 1)
            act.wait_ge(w_in, 16 * 8)
            act.wait_ge(ones_ok, 6)
            scaled(A, 0, 0, 0, 0)
            for k in range(KC):
                tokens_high(0, 0, k)
            for c in range(2):
                order_heads(act.copy, wkx_hi, wkv_sb, c, w_high_a)
            for k in range(KC):
                act.copy(wvx_hi[:, k, :], wkv_sb[:, k, D:2 * D]).then_inc(w_high_a, 1)
            with act.Fori(0, B - 1) as b:
                dense_a(b, True)
            dense_a(B - 1, False)

            def attention(a, ahead):
                def slot(q, b):
                    v0, s = q // a.NS, q % a.NS
                    if v0 >= 4 * B:
                        return
                    v = v0 + 4 * b
                    n = a.steps[s][3]
                    step = a.NS * v + s
                    act.wait_ge(a.pv_done, step + 1)
                    for i in range(4):
                        act.wait_ge(a.st_ready, 4 * step + i + 1)
                        use = 4 * (a.NS * v0 + s) + i
                        act.activation(probs[0:a.kp, use % NPT, 0:n], bank[0:a.kp, a.s_banks[use % a.SB], 0:n], ACT.Exp,
                                       scale=SCALE).then_inc(a.exp_done, 1)
                    if v0 >= 4 * B - 2:
                        ahead(q - (4 * B - 2) * a.NS)

                sequence(act, a, slot)

            act.wait_ge(A.parts_ready, 10 * B)
            for s in range(4):
                act.wait_ge(A.parts_stored[s], 16 + 16 * 2 * B)
            attention(SA, lambda step: None)

            for dst, src in ((w1_sb, w1), (w2_sb, w2)):
                act.dma_start(dst[:, :, :], src.rearrange("(k p) n -> p k n", p=P)).then_inc(w_ffn, 16)

            with act.Fori(0, B) as b:
                for hf in range(2):
                    n = 2 * b + hf
                    scaled(C, 1, n, hf, 6)
                    for c in range(2):
                        act.wait_ge(C.parts_stored[c], 16 * n + 16)
                        high(C, 2 * n + c, parts[:, c, 0, :], bank[:, c, :])
                    for c in range(2):
                        middle(C, 2, 2 * n + c, parts[:, c, 1, :], rest[:, c])

            def context_high(b, hf):
                act.wait_ge(c_in[hf], 16 * b + 16)
                act.copy(cT_hi[:, hf], cT[:, hf]).then_inc(c_hi, 1)

            def ahead_e(step):
                if step == 0:
                    act.wait_ge(XA.st_ready, 4 * XA.NS * (4 * B - 3))
                    context_high(0, 0)

            attention(XA, ahead_e)

            def scaled_e(n, hf, b0=2):
                scaled(E, 2, n, hf, b0)
                for k in range(KC):
                    act.wait_ge(E.nxT_ready, 2 * n + k + 1)
                    act.copy(nT_hi[:, hf, k, :], nxT[:, hf, k, :]).then_inc(nxT_high, 1)

            def dense_e(b, more):
                for hf in range(2):
                    n = 2 * b + hf
                    for f in range(FC):
                        act.wait_ge(h_ready, FC * n + f + 1)
                        act.wait_ge(h_lo, FC * n + f + 1)
                        act.activation(hT[:, f % HRING, :], bank[:, f % 2, :], ACT.Relu, bias=b1_sb[:, f:f + 1]).then_inc(h_evac, 1)
                        if f == 1 and (hf == 0 or more):
                            context_high(b + hf, 1 - hf)
                    if hf == 0 or more:
                        scaled_e(n + 1, 1 - hf)

            scaled_e(0, 0, 6)
            with act.Fori(0, B - 1) as b:
                dense_e(b, True)
            dense_e(B - 1, False)

        @block.vector
        def _(dve):
            fill_stacks(dve, 0, ones_ok)
            dve.memset(vst[:, :, :, :, DK:NV].rearrange("p a t h e -> p (a t h) e"), 1.0).then_inc(ones_ok, 1)
            dve.memset(vstx[:, :, :, DK:NV].rearrange("p k h e -> p (k h) e"), 1.0).then_inc(ones_ok, 1)
            dve.memset(mx[:, :, :, :].rearrange("p a b c -> p (a b c)"), LOWEST).then_inc(ones_ok, 1)
            dve.memset(nx_mem[:, 2 * VCOLS - 32 + NV:2 * VCOLS], 0.0).then_inc(ones_ok, 1)

            for ph, k in ((A, 10), (C, 2)):
                dve.sem_inc(ph.rest_ready, k)
            for ph in (C, E):
                dve.sem_inc(ph.xn_done, 2)
            dve.sem_inc(y_done, 2)
            for a in (SA, XA):
                dve.sem_inc(a.acc_free, 2)
                for hf in range(2):
                    dve.sem_inc(a.oC_ready[hf], 1)

            def moments(ph, src, n, hf):
                for t in range(TT):
                    last = dve.bn_stats(stats[:, hf, t, :], src[:, hf, t, :])
                last.then_inc(ph.stat_done, 1)
                dve.wait_ge(ph.stat_done, n + 1)
                dve.sem_inc(ph.stat_seen, 1)
                for t in range(TT):
                    last = dve.bn_aggr(mv[:, hf, t, :], stats[:, hf, t, :])
                last.then_inc(ph.var_ready, 1)

            def normalize(ph, src, n, hf):
                dve.wait_ge(ph.rstd_ready, n + 1)
                for t in range(TT):
                    last = dve.tensor_scalar(nx[:, hf, t, :], src[:, hf, t, :], mv[:, hf, t, 0:1], rstd[:, hf, t:t + 1],
                                             ALU.subtract, ALU.mult)
                last.then_inc(ph.nx_ready, 1)

            def split(ph, use, dst, src, hi):
                dve.wait_ge(ph.hi_ready, use + 1)
                dve.tensor_tensor(dst, src, hi, ALU.subtract).then_inc(ph.rest_ready, 1)

            def max_tile(a, v0, b, n, ring):
                v, par = v0 + 4 * b, v0 % 2
                blocks, _, keys, part = a.tiles[n]
                use, m = a.tile_use(v, n), a.m_banks[a.tile_use(v0, n) % ring]
                dve.wait_ge(a.m_ready, use + 1)
                dve.tensor_reduce(mx[:, par, part, blocks.start:blocks[-1] + 1:blocks.step],
                                  bank[:, m, 0:len(blocks) * keys].rearrange("p (q k) -> p q k", k=keys), AX.X, ALU.max
                                  ).then_inc(a.m_free, 1)
                if a.causal and n == a.MT - 1:
                    dve.wait_ge(a.m_free, use + 1)
                    dve.tensor_tensor(mxc[:, par], mx[:, par, 0], mx[:, par, 1], ALU.max).then_inc(a.mxc_ready, 1)

            def negate(a, v0, b, ring):
                v = v0 + 4 * b
                use, m = a.turn_use(v0) + 4 * b * (a.MT + 1), a.m_banks[a.turn_use(v0) % ring]
                if v0:
                    dve.wait_ge(a.nm_ready, v)
                dve.wait_ge(a.m_ready, use + 1)
                dve.tensor_scalar(nmf[:, :], bank[0:32, m, 0:P], -1.0, None, ALU.mult).then_inc(a.m_free, 1)

            def first_tiles(a, tiles, ring):
                for v, n in tiles:
                    max_tile(a, v, 0, n, ring)
                    if v == 1 and n == a.M0 - 1:
                        negate(a, 0, 0, ring)

            def moments_a(b, hf):
                dve.wait_ge(A.x_in[hf], 16 * b + 16)
                moments(A, xt, 2 * b + hf, hf)

            def tokens_low(n, hf, k):
                dve.wait_ge(nxT_high_a, KC * n + k + 1)
                dve.tensor_tensor(nxT_lo[:, hf, k, :], nxT[:, hf, k, :], nxT_hi[:, hf, k, :].bitcast(F32),
                                  ALU.subtract).then_inc(nxT_low_a, 1)

            def dense_a(b, more, early=None):
                def between(hf, j):
                    if early:
                        first_tiles(SA, early[EARLY_SLOTS * hf + j], EARLY_BANKS)

                for hf in range(2):
                    n = 2 * b + hf
                    if more:
                        moments_a(b + 1, hf)
                    for s in range(4):
                        for j in range(2):
                            between(hf, (2 * s if s < 3 else 8) + j)
                        split(A, 10 * b + 4 * hf + s, rest[:, s], bank[:, 2 + s % 2, :], parts[:, s, 0, :])
                        if s in (1, 2) and (hf == 0 or more):
                            tokens_low(n + 1, 1 - hf, s - 1)
                        if s == 1 and more:
                            normalize(A, xt, n + 2, hf)
                        if s == 2:
                            for j in range(2):
                                between(hf, 6 + j)
                    if hf == 0:
                        dve.wait_ge(cxT_high, b + 1)
                        dve.tensor_tensor(cxT_lo[:, :, :], cxT[:, :, :], cxT_hi[:, :, :].bitcast(F32), ALU.subtract).then_inc(cxT_low, 1)
                    for j in range(2):
                        between(hf, 10 + j)
                for c in range(2):
                    split(A, 10 * b + 8 + c, restx[:, c], bank[:, 2 + c, 0:LX], partsx[:, c, 0, :])

            moments_a(0, 0)
            normalize(A, xt, 0, 0)
            moments_a(0, 1)
            for k in range(KC):
                tokens_low(0, 0, k)
            normalize(A, xt, 1, 1)
            with dve.Fori(0, B - 2) as b:
                dense_a(b, True)
            dense_a(B - 2, True, early_slots[:2 * EARLY_SLOTS])
            dense_a(B - 1, False, early_slots[2 * EARLY_SLOTS:])

            def attention(a, ahead):
                def turn_sums(v0, b, hf):
                    v = v0 + 4 * b
                    dve.wait_ge(a.oN_done, 2 + 2 * v + hf - 1)
                    dve.wait_ge(a.pv_done, PROBS_STEPS + a.NS * v + a.last[hf] + 1)
                    dve.transpose(oT[:, hf].rearrange("p c d -> p (c d)"), bank[:, a.acc[hf % a.AB], :]).then_inc(a.acc_free, 1)

                def invert(v0, b, hf):
                    n = 2 * (v0 + 4 * b) + hf
                    dve.wait_ge(a.acc_free, 2 + n + 1)
                    dve.reciprocal(rs[:, hf, :], oT[:, hf, :, DK]).then_inc(a.rs_done, 1)

                def turn_back(v0, b, hf):
                    v, u = v0 + 4 * b, v0 // 2 + 2 * b
                    dve.wait_ge(a.oN_done, 2 + 2 * v + hf + 1)
                    dve.wait_ge(a.oC_stored[hf], 16 * u + 16)
                    dve.transpose(oC[:, hf, :], oN[:, hf].rearrange("p c d -> p (c d)")).then_inc(a.oC_ready[hf], 1)

                def slot(q, b):
                    v0, s = q // a.NS, q % a.NS
                    some = a.beside[s] if v0 + 2 < 4 * B else []
                    cut = len(some) - len(some) // 2
                    for n in some[:cut]:
                        max_tile(a, v0 + 2, b, n, a.MB)
                    if s == 0 and v0 + 1 < 4 * B:
                        negate(a, v0 + 1, b, a.MB)
                    for hf in range(2):
                        v1, s1 = divmod(q - LAG, a.NS)
                        if 0 <= v1 < 4 * B and s1 == a.last[hf]:
                            turn_sums(v1, b, hf)
                        v1, s1 = divmod(q - TAIL, a.NS)
                        if v1 >= 0 and v1 % 2 and s1 == a.last[hf]:
                            turn_back(v1, b, hf)
                    for n in some[cut:]:
                        max_tile(a, v0 + 2, b, n, a.MB)
                    for hf in range(2):
                        v1, s1 = divmod(q - LAG, a.NS)
                        if 0 <= v1 < 4 * B and s1 == a.last[hf]:
                            invert(v1, b, hf)
                    if v0 >= 4 * B - 2:
                        ahead(q - (4 * B - 2) * a.NS)

                if a is XA:
                    first_tiles(a, [(v, n) for v in range(2) for n in range(a.MT)], a.MB)
                sequence(dve, a, slot)

            def weights_split(w, hi, lo, n):
                dve.tensor_copy(hi[:, :, :], w[:, :, :]).then_inc(w_high, 1)
                dve.wait_ge(w_high, n)
                dve.tensor_tensor(lo[:, :, :], w[:, :, :], hi[:, :, :].bitcast(F32), ALU.subtract).then_inc(w_low, 1)

            def residual(ph, b, hf, o_bank, per):
                n = 2 * b + hf
                dve.wait_ge(ph.x_in[hf], per * b + per)
                for i in range(2):
                    dve.wait_ge(ph.o_ready, 2 * n + i + 1)
                    dve.tensor_tensor(xn[:, hf, 2 * i:2 * i + 2, :], xt[:, hf, 2 * i:2 * i + 2, :],
                                      bank[:, o_bank + i, :].rearrange("p (t d) -> p t d", t=2), ALU.add).then_inc(ph.xn_done, 1)
                dve.wait_ge(ph.xn_done, 2 + 2 * n + 2)
                moments(ph, xn, n, hf)

            def sums_c(b, hf):
                dve.wait_ge(x1_stored[hf], 16 * b + 16)
                residual(C, b, hf, 4, 32)

            def ahead_c(step):
                if step in (9, 17):
                    sums_c(0, step // 16)
                if step == 15:
                    dve.wait_ge(SA.pv_done, PROBS_STEPS + (4 * B - 2) * SA.NS)
                    normalize(C, xn, 0, 0)

            attention(SA, ahead_c)

            def dense_c(b, more):
                for hf in range(2):
                    n = 2 * b + hf
                    if hf == 0 or more:
                        normalize(C, xn, n + 1, 1 - hf)
                    if more:
                        sums_c(b + 1, hf)
                    for c in range(2):
                        split(C, 2 * n + c, rest[:, c], bank[:, c, :], parts[:, c, 0, :])

            dve.wait_ge(SA.pv_done, PROBS_STEPS + 4 * B * SA.NS)
            with dve.Fori(0, B - 1) as b:
                dense_c(b, True)
            dense_c(B - 1, False)

            weights_split(wco_sb, wco_hi, wco_lo, 1)
            def context_low(n, hf):
                dve.wait_ge(c_hi, n + 1)
                dve.tensor_tensor(cT_lo[:, hf], cT[:, hf], cT_hi[:, hf].bitcast(F32), ALU.subtract).then_inc(c_lo, 1)

            def scaled_low(n, hf):
                for k in range(KC):
                    dve.wait_ge(nxT_high, 2 * n + k + 1)
                    dve.tensor_tensor(nT_lo[:, hf, k, :], nxT[:, hf, k, :], nT_hi[:, hf, k, :].bitcast(F32),
                                      ALU.subtract).then_inc(nxT_low, 1)

            def sums_e(b, hf, o_bank=4):
                dve.wait_ge(y_stored[hf], 16 * b + 16)
                residual(E, b, hf, o_bank, 16)

            def ahead_e(step):
                if step == 1:
                    context_low(0, 0)
                if step == 3:
                    sums_e(0, 0, 6)
                if step == 4:
                    dve.wait_ge(XA.pv_done, PROBS_STEPS + (4 * B - 2) * XA.NS)
                    normalize(E, xn, 0, 0)
                if step == 5:
                    dve.wait_ge(w_ffn, 16 * 2)
                    dve.wait_ge(XA.st_ready, 4 * XA.NS * (4 * B - 1))
                    weights_split(w1_sb, w1_hi, w1_lo, 2)
                if step == 2 * XA.NS + 1:
                    scaled_low(0, 0)

            attention(XA, ahead_e)

            def dense_e(b, more):
                for hf in range(2):
                    n = 2 * b + hf
                    for f in range(FC):
                        dve.wait_ge(h_evac, 2 + FC * n + f + 1)
                        dve.tensor_copy(hT_hi[:, f, :], hT[:, f % HRING, :]).then_inc(h_hi, 1)
                        if f == 2 and (hf == 0 or more):
                            context_low(n + 1, 1 - hf)
                    if hf == 0 or more:
                        sums_e(b + hf, 1 - hf)
                        normalize(E, xn, n + 1, 1 - hf)
                        scaled_low(n + 1, 1 - hf)
                    dve.wait_ge(xb_ready, n + 1)
                    for i in range(2):
                        dve.wait_ge(f_ready, 2 * n + i + 1)
                        dve.tensor_tensor(xn[:, hf, 2 * i:2 * i + 2, :], xt[:, hf, 2 * i:2 * i + 2, :],
                                          bank[:, 6 + i, :].rearrange("p (t d) -> p t d", t=2), ALU.add).then_inc(y_done, 1)

            dve.wait_ge(XA.st_ready, 4 * XA.NS * 4 * B)
            weights_split(w2_sb, w2_hi, w2_lo, 3)
            dve.wait_ge(XA.pv_done, PROBS_STEPS + 4 * B * XA.NS)
            with dve.Fori(0, B - 1) as b:
                dense_e(b, True)
            dense_e(B - 1, False)

        @block.gpsimd
        def _(pool):
            fill_stacks(pool, 1, st_filled)
            pool.wait_ge(st_filled, 2)
            pool.memset(ident[:, :], 0.0).then_inc(pool_const, 1)
            pool.memset(ident_bf[:, :], 0.0).then_inc(pool_const, 1)
            pool.memset(causal_bf[:, :], 0.0).then_inc(pool_const, 1)
            pool.memset(minus_half[:, :], -0.5).then_inc(pool_const, 1)
            pool.memset(eps_sb[:, :], EPS).then_inc(pool_const, 1)
            pool.memset(zeros[:, :], 0.0).then_inc(pool_const, 1)
            pool.wait_ge(pool_const, 6)
            for t in (ident, ident_bf):
                pool.affine_select(out=t[:, :], in_=t[:, :], compare_op=ALU.not_equal, fill=1.0, base=0,
                                   pattern=[[1, P]], channel_multiplier=-1).then_inc(consts_ok, 1)
            pool.affine_select(out=causal_bf[:, :], in_=causal_bf[:, :], compare_op=ALU.is_ge, fill=MASKED, base=0,
                               pattern=[[-1, P]], channel_multiplier=1).then_inc(consts_ok, 1)

            def deviation(ph, n, hf):
                pool.wait_ge(ph.var_ready, n + 1)
                pool.tensor_tensor(veps[:, hf, :], mv[:, hf, :, 1], eps_sb[:, :], ALU.add).then_inc(ph.eps_done, 1)
                pool.wait_ge(ph.eps_done, n + 1)
                pool.tensor_tensor(rstd[:, hf, :], veps[:, hf, :], minus_half[:, :], ALU.pow).then_inc(ph.rstd_ready, 1)

            def lowest(ph, use, src, mid, low):
                pool.wait_ge(ph.mid_done, use + 1)
                pool.tensor_tensor(low, src, mid, ALU.subtract).then_inc(ph.parts_ready, 1)

            def negated_parts(a, v0, b):
                v, par = v0 + 4 * b, v0 % 2
                if v0 >= 2:
                    pool.wait_ge(a.rows_in[par], 16 * (v0 // 2 + 2 * b))
                pool.wait_ge(a.m_free, a.turn_use(v0) + 4 * b * (a.MT + 1) + 1)
                pool.tensor_tensor(nm[:, par, 0, :], nmf[:, :], zeros[:, :], ALU.add).then_inc(a.nm_hi, 1)
                pool.wait_ge(a.nm_hi, v + 1)
                pool.tensor_tensor(nmr[:, :], nmf[:, :], nm[:, par, 0, :], ALU.subtract).then_inc(a.nmr_done, 1)
                pool.wait_ge(a.nmr_done, v + 1)
                pool.tensor_tensor(nm[:, par, 1, :], nmr[:, :], zeros[:, :], ALU.add).then_inc(a.nm_mid, 1)
                pool.wait_ge(a.nm_mid, v + 1)
                pool.tensor_tensor(nm[:, par, 2, :], nmr[:, :], nm[:, par, 1, :], ALU.subtract).then_inc(a.nm_ready, 1)

            def dense_a(b, more):
                for hf in range(2):
                    if more:
                        deviation(A, 2 * (b + 1) + hf, hf)
                    for s in range(4):
                        lowest(A, 10 * b + 4 * hf + s, rest[:, s], parts[:, s, 1, :], parts[:, s, 2, :])
                    if not more and hf == 0:
                        negated_parts(SA, 0, 0)
                for c in range(2):
                    lowest(A, 10 * b + 8 + c, restx[:, c], partsx[:, c, 1, :], partsx[:, c, 2, :])

            def weights_low(lo, raw, hi, use):
                pool.wait_ge(w_high_a, use + 1)
                pool.tensor_tensor(lo, raw, hi.bitcast(F32), ALU.subtract).then_inc(w_low_a, 1)

            def heads_low(lo, raw, hi, c, use):
                for k in range(KC):
                    weights_low(lo[:, k, P * c:P * c + P].rearrange("p (g d i) -> p g d i", g=2, d=DK),
                                raw[:, k, P * c:P * c + P].rearrange("p (i g d) -> p g d i", g=2, d=DK),
                                hi[:, k, P * c:P * c + P].rearrange("p (g d i) -> p g d i", g=2, d=DK), use + k)

            for c in range(4):
                heads_low(wqk_lo, wqkv_sb, wqk_hi, c, KC * c)
                if c in (1, 3):
                    deviation(A, c // 2, c // 2)
            for k in range(KC):
                weights_low(wv_lo[:, k, :], wqkv_sb[:, k, 2 * D:3 * D], wv_hi[:, k, :], KC * 4 + k)
            for c in range(2):
                heads_low(wkx_lo, wkv_sb, wkx_hi, c, KC * (5 + c))
            for k in range(KC):
                weights_low(wvx_lo[:, k, :], wkv_sb[:, k, D:2 * D], wvx_hi[:, k, :], KC * 7 + k)
            pool.wait_ge(w_low_a, KC * 8)
            fill_stacks(pool, 2, st_filled)
            pool.wait_ge(st_filled, 4)
            with pool.Fori(0, B - 1) as b:
                dense_a(b, True)
            dense_a(B - 1, False)

            pool.wait_ge(A.parts_ready, 10 * B)
            pool.wait_ge(v_evac, 2 + 5 * B)
            fill_stacks(pool, 3, st_filled)
            pool.wait_ge(st_filled, 6)
            pool.wait_ge(w_late, 16 * 4)
            for c in range(2):
                order_heads(pool.tensor_copy, wqx_sb, wq_sb, c, w_ordered)

            for a in (SA, XA):
                pool.sem_inc(a.oN_done, 2)

            def attention(a, ahead):
                def mask(v0, b, s):
                    for p in range(2):
                        use = 4 * (a.NS * v0 + s) + 2 * p
                        pool.wait_ge(a.exp_done, a.SB + use + 2 + 4 * b * 4 * a.NS)
                        pool.sem_inc(a.exp_seen, 1)
                        tri = probs[:, use % NPT:use % NPT + 2, 0:P]
                        pool.affine_select(out=tri, in_=tri, compare_op=ALU.is_ge, fill=0.0, base=0,
                                           pattern=[[0, 2], [1, P]], channel_multiplier=-1).then_inc(a.mask_done, 1)

                def divide(v0, b, hf):
                    v, g, u = v0 + 4 * b, v0 % 2, v0 // 2 + 2 * b
                    if not g:
                        pool.wait_ge(a.oC_ready[hf], 1 + u)
                    pool.wait_ge(a.rs_done, 2 * v + hf + 1)
                    pool.tensor_tensor(oN[:, hf, :, DK * g:DK * g + DK], oT[:, hf, :, 0:DK],
                                       rs[:, hf, :].unsqueeze(2).to_broadcast([P, 16, DK]), ALU.mult).then_inc(a.oN_done, 1)

                def slot(q, b):
                    v0, s = q // a.NS, q % a.NS
                    for hf in range(2):
                        v1, s1 = divmod(q - LAG, a.NS)
                        if 0 <= v1 < 4 * B and s1 == a.last[hf]:
                            divide(v1, b, hf)
                    if v0 < 4 * B and s in a.diag:
                        mask(v0, b, s)
                    if s == 0 and v0 + 1 < 4 * B:
                        negated_parts(a, v0 + 1, b)
                    if v0 >= 4 * B - 2:
                        ahead(q - (4 * B - 2) * a.NS)

                if a is XA:
                    negated_parts(a, 0, 0)
                sequence(pool, a, slot)

            def ahead_c(step):
                if step in (11, 19):
                    deviation(C, step // 16, step // 16)

            attention(SA, ahead_c)

            def dense_c(b, more):
                for hf in range(2):
                    n = 2 * b + hf
                    if more:
                        deviation(C, n + 2, hf)
                    for c in range(2):
                        lowest(C, 2 * n + c, rest[:, c], parts[:, c, 1, :], parts[:, c, 2, :])

            with pool.Fori(0, B - 1) as b:
                dense_c(b, True)
            dense_c(B - 1, False)

            def biased_e(n, hf):
                deviation(E, n, hf)
                pool.wait_ge(E.xn_done, 2 + 2 * n + 2)
                pool.tensor_tensor(xt[:, hf], xn[:, hf], b2_sb[:, :].unsqueeze(1).to_broadcast([P, TT, D]),
                                   ALU.add).then_inc(xb_ready, 1)

            def ahead_e(step):
                if step == 4:
                    biased_e(0, 0)

            attention(XA, ahead_e)

            def dense_e(b, more):
                for hf in range(2):
                    n = 2 * b + hf
                    for f in range(FC):
                        pool.wait_ge(h_hi, FC * n + f + 1)
                        pool.tensor_tensor(hT_lo[:, f, :], hT[:, f % HRING, :], hT_hi[:, f, :].bitcast(F32), ALU.subtract).then_inc(h_lo, 1)
                    if hf == 0 or more:
                        biased_e(n + 1, 1 - hf)

            pool.sem_inc(h_lo, HRING)
            with pool.Fori(0, B - 1) as b:
                dense_e(b, True)
            dense_e(B - 1, False)


_PRE = "L0_xattn_"
_INS = ["x", "ctx_1024"] + [_PRE + n for n in (
    "W_qkv", "W_self_out", "W_q", "W_kv", "W_cross_out", "W1", "b1", "W2", "b2",
    "ln1_scale", "ln1_bias", "ln2_scale", "ln2_bias", "ln3_scale", "ln3_bias")]


def kernel(**inputs):
    import numpy as _np
    import concourse.bacc as _bacc
    from concourse import mybir as _mybir
    from concourse.bass_utils import run_bass_kernel_spmd as _run

    nc = _bacc.Bacc("TRN2", target_bir_lowering=False, num_devices=1)
    arrays, args = {}, []
    for name in _INS:
        a = _np.ascontiguousarray(inputs[name])
        arrays[f"in_{name}_dram"] = a
        args.append(nc.dram_tensor(f"in_{name}_dram", a.shape, _mybir.dt.from_np(a.dtype), kind="ExternalInput").ap())
    shape = arrays["in_x_dram"].shape
    args.append(nc.dram_tensor("out_0_dram", shape, _mybir.dt.float32, kind="ExternalOutput").ap())
    decoder_block_kernel(nc, *args)
    r = _run(nc, [arrays], core_ids=[0])
    return r.results[0]["out_0_dram"]
```
